# Optimizing a Trainium2 kernel written in Bass

```python
import numpy as np
import jax
import jax.numpy as jnp

def _softmax(x, axis=-1):
    return jax.nn.softmax(x, axis=axis)

def _gelu(x):
    return jax.nn.gelu(x, approximate=True)

def _silu(x):
    return jax.nn.silu(x)

def _sigmoid(x):
    return jax.nn.sigmoid(x)

def _layernorm(x, axis=-1, eps=1e-05):
    m = jnp.mean(x, axis=axis, keepdims=True)
    v = jnp.var(x, axis=axis, keepdims=True)
    return (x - m) / jnp.sqrt(v + eps)

def _scatter_add(tgt, idx, src, axis=0):
    return tgt.at[idx].add(src)

def _segment_sum(src, seg, n):
    return jax.ops.segment_sum(src, seg, n)
kernel_name = 'mk_seq_postln_d1_jaxref_r8_92af12'

def setup_inputs(seed: int=0):
    np.random.seed(seed)
    _w = jnp.asarray

    def _L0_attn_setup():
        import jax, jax.numpy as jnp
        import numpy as np
        from functools import partial
        D_MODEL = 128
        D_STATE = 16
        D_CONV = 4
        EXPAND = 2
        D_INNER = EXPAND * D_MODEL
        DT_RANK = (D_MODEL + 15) // 16
        BATCH, SEQ = (2, 128)

        def _mamba_params(key):
            ks = jax.random.split(key, 9)
            s = lambda k, shape, scale: jax.random.normal(k, shape, jnp.float32) * scale
            return dict(in_w=s(ks[0], (2 * D_INNER, D_MODEL), D_MODEL ** (-0.5)), conv_w=s(ks[1], (D_INNER, 1, D_CONV), D_CONV ** (-0.5)), conv_b=s(ks[2], (D_INNER,), 0.02), xproj_w=s(ks[3], (DT_RANK + 2 * D_STATE, D_INNER), D_INNER ** (-0.5)), dt_w=s(ks[4], (D_INNER, DT_RANK), DT_RANK ** (-0.5)), dt_b=s(ks[5], (D_INNER,), 0.02), A_log=jnp.log(jnp.broadcast_to(jnp.arange(1, D_STATE + 1, dtype=jnp.float32), (D_INNER, D_STATE))), D=jnp.ones((D_INNER,), jnp.float32), out_w=s(ks[8], (D_MODEL, D_INNER), D_INNER ** (-0.5)))

        def _mamba(x, in_w, conv_w, conv_b, xproj_w, dt_w, dt_b, A_log, D, out_w):
            B, L, _ = x.shape
            xz = jnp.einsum('bld,ed->ble', x, in_w)
            u, z = jnp.split(xz, 2, axis=-1)
            u_c = jnp.swapaxes(u, 1, 2)
            u_c = jax.lax.conv_general_dilated(u_c, conv_w, window_strides=(1,), padding=[(D_CONV - 1, 0)], dimension_numbers=('NCH', 'OIH', 'NCH'), feature_group_count=D_INNER)
            u_c = u_c + conv_b[None, :, None]
            u = jax.nn.silu(jnp.swapaxes(u_c, 1, 2))
            x_dbl = jnp.einsum('bld,ed->ble', u, xproj_w)
            dt = jax.nn.softplus(jnp.einsum('blr,dr->bld', x_dbl[..., :DT_RANK], dt_w) + dt_b)
            Bm = x_dbl[..., DT_RANK:DT_RANK + D_STATE]
            Cm = x_dbl[..., DT_RANK + D_STATE:]
            A = -jnp.exp(A_log)
            dA = jnp.exp(dt[..., None] * A)
            dBu = dt[..., None] * Bm[:, :, None, :] * u[..., None]

            def step(h, ins):
                dA_t, dBu_t, C_t = ins
                h = dA_t * h + dBu_t
                y = jnp.einsum('bdn,bn->bd', h, C_t)
                return (h, y)
            h0 = jnp.zeros((B, D_INNER, D_STATE), dA.dtype)
            _, ys = jax.lax.scan(step, h0, (jnp.swapaxes(dA, 0, 1), jnp.swapaxes(dBu, 0, 1), jnp.swapaxes(Cm, 0, 1)))
            y = jnp.swapaxes(ys, 0, 1) + u * D
            y = y * jax.nn.silu(z)
            return jnp.einsum('bld,ed->ble', y, out_w)
        key = jax.random.key(seed)
        kx, kf, kb, kg = jax.random.split(key, 4)
        inp = {'x': jax.random.normal(kx, (BATCH, SEQ, D_MODEL), jnp.float32), 'gamma': jnp.ones((D_MODEL,), jnp.float32), 'beta': jnp.zeros((D_MODEL,), jnp.float32)}
        for pref, k in (('f_', kf), ('b_', kb)):
            for name, val in _mamba_params(k).items():
                inp[pref + name] = val
        return inp
    _L0_attn_in = _L0_attn_setup()

    def _L0_ffn_setup():
        import jax, jax.numpy as jnp
        import numpy as np
        NUM_EXPERTS = 8
        TOP_K = 2
        D_MODEL = 128
        D_HID = 512
        BATCH, SEQ = (2, 256)
        key = jax.random.key(seed)
        ks = jax.random.split(key, 5)
        s = 0.02
        return {'x': jax.random.normal(ks[0], (BATCH, SEQ, D_MODEL), dtype=jnp.float32), 'Wg': jax.random.normal(ks[1], (D_MODEL, NUM_EXPERTS), dtype=jnp.float32) * s, 'bg': jnp.zeros((NUM_EXPERTS,), dtype=jnp.float32), 'W0': jax.random.normal(ks[2], (NUM_EXPERTS, D_MODEL, D_HID), dtype=jnp.float32) * s, 'b0': jnp.zeros((NUM_EXPERTS, D_HID), dtype=jnp.float32), 'W1': jax.random.normal(ks[3], (NUM_EXPERTS, D_MODEL, D_HID), dtype=jnp.float32) * s, 'b1': jnp.zeros((NUM_EXPERTS, D_HID), dtype=jnp.float32), 'W2': jax.random.normal(ks[4], (NUM_EXPERTS, D_HID, D_MODEL), dtype=jnp.float32) * s, 'b2': jnp.zeros((NUM_EXPERTS, D_MODEL), dtype=jnp.float32)}
    _L0_ffn_in = _L0_ffn_setup()
    _d = {'L0_attn_x': _L0_attn_in['x'], 'L0_attn_gamma': _L0_attn_in['gamma'], 'L0_attn_beta': _L0_attn_in['beta'], 'L0_attn_f_in_w': _L0_attn_in['f_in_w'], 'L0_attn_f_conv_w': _L0_attn_in['f_conv_w'], 'L0_attn_f_conv_b': _L0_attn_in['f_conv_b'], 'L0_attn_f_xproj_w': _L0_attn_in['f_xproj_w'], 'L0_attn_f_dt_w': _L0_attn_in['f_dt_w'], 'L0_attn_f_dt_b': _L0_attn_in['f_dt_b'], 'L0_attn_f_A_log': _L0_attn_in['f_A_log'], 'L0_attn_f_D': _L0_attn_in['f_D'], 'L0_attn_f_out_w': _L0_attn_in['f_out_w'], 'L0_attn_b_in_w': _L0_attn_in['b_in_w'], 'L0_attn_b_conv_w': _L0_attn_in['b_conv_w'], 'L0_attn_b_conv_b': _L0_attn_in['b_conv_b'], 'L0_attn_b_xproj_w': _L0_attn_in['b_xproj_w'], 'L0_attn_b_dt_w': _L0_attn_in['b_dt_w'], 'L0_attn_b_dt_b': _L0_attn_in['b_dt_b'], 'L0_attn_b_A_log': _L0_attn_in['b_A_log'], 'L0_attn_b_D': _L0_attn_in['b_D'], 'L0_attn_b_out_w': _L0_attn_in['b_out_w'], 'L0_ffn_Wg': _L0_ffn_in['Wg'], 'L0_ffn_bg': _L0_ffn_in['bg'], 'L0_ffn_W0': _L0_ffn_in['W0'], 'L0_ffn_b0': _L0_ffn_in['b0'], 'L0_ffn_W1': _L0_ffn_in['W1'], 'L0_ffn_b1': _L0_ffn_in['b1'], 'L0_ffn_W2': _L0_ffn_in['W2'], 'L0_ffn_b2': _L0_ffn_in['b2']}
    _x0 = _d['L0_attn_x']
    _d['L0_attn_x'] = jax.random.normal(jax.random.fold_in(jax.random.key(seed), 1), (8, 1024, 128), dtype=_x0.dtype)
    del _x0
    return _d

def reference(L0_attn_x, L0_attn_gamma, L0_attn_beta, L0_attn_f_in_w, L0_attn_f_conv_w, L0_attn_f_conv_b, L0_attn_f_xproj_w, L0_attn_f_dt_w, L0_attn_f_dt_b, L0_attn_f_A_log, L0_attn_f_D, L0_attn_f_out_w, L0_attn_b_in_w, L0_attn_b_conv_w, L0_attn_b_conv_b, L0_attn_b_xproj_w, L0_attn_b_dt_w, L0_attn_b_dt_b, L0_attn_b_A_log, L0_attn_b_D, L0_attn_b_out_w, L0_ffn_Wg, L0_ffn_bg, L0_ffn_W0, L0_ffn_b0, L0_ffn_W1, L0_ffn_b1, L0_ffn_W2, L0_ffn_b2):

    def _L0_attn_ref(x, gamma, beta, f_in_w, f_conv_w, f_conv_b, f_xproj_w, f_dt_w, f_dt_b, f_A_log, f_D, f_out_w, b_in_w, b_conv_w, b_conv_b, b_xproj_w, b_dt_w, b_dt_b, b_A_log, b_D, b_out_w):
        import jax, jax.numpy as jnp
        import numpy as np
        from functools import partial
        D_MODEL = 128
        D_STATE = 16
        D_CONV = 4
        EXPAND = 2
        D_INNER = EXPAND * D_MODEL
        DT_RANK = (D_MODEL + 15) // 16
        BATCH, SEQ = (2, 128)

        def _mamba_params(key):
            ks = jax.random.split(key, 9)
            s = lambda k, shape, scale: jax.random.normal(k, shape, jnp.float32) * scale
            return dict(in_w=s(ks[0], (2 * D_INNER, D_MODEL), D_MODEL ** (-0.5)), conv_w=s(ks[1], (D_INNER, 1, D_CONV), D_CONV ** (-0.5)), conv_b=s(ks[2], (D_INNER,), 0.02), xproj_w=s(ks[3], (DT_RANK + 2 * D_STATE, D_INNER), D_INNER ** (-0.5)), dt_w=s(ks[4], (D_INNER, DT_RANK), DT_RANK ** (-0.5)), dt_b=s(ks[5], (D_INNER,), 0.02), A_log=jnp.log(jnp.broadcast_to(jnp.arange(1, D_STATE + 1, dtype=jnp.float32), (D_INNER, D_STATE))), D=jnp.ones((D_INNER,), jnp.float32), out_w=s(ks[8], (D_MODEL, D_INNER), D_INNER ** (-0.5)))

        def _mamba(x, in_w, conv_w, conv_b, xproj_w, dt_w, dt_b, A_log, D, out_w):
            B, L, _ = x.shape
            xz = jnp.einsum('bld,ed->ble', x, in_w)
            u, z = jnp.split(xz, 2, axis=-1)
            u_c = jnp.swapaxes(u, 1, 2)
            u_c = jax.lax.conv_general_dilated(u_c, conv_w, window_strides=(1,), padding=[(D_CONV - 1, 0)], dimension_numbers=('NCH', 'OIH', 'NCH'), feature_group_count=D_INNER)
            u_c = u_c + conv_b[None, :, None]
            u = jax.nn.silu(jnp.swapaxes(u_c, 1, 2))
            x_dbl = jnp.einsum('bld,ed->ble', u, xproj_w)
            dt = jax.nn.softplus(jnp.einsum('blr,dr->bld', x_dbl[..., :DT_RANK], dt_w) + dt_b)
            Bm = x_dbl[..., DT_RANK:DT_RANK + D_STATE]
            Cm = x_dbl[..., DT_RANK + D_STATE:]
            A = -jnp.exp(A_log)
            dA = jnp.exp(dt[..., None] * A)
            dBu = dt[..., None] * Bm[:, :, None, :] * u[..., None]

            def step(h, ins):
                dA_t, dBu_t, C_t = ins
                h = dA_t * h + dBu_t
                y = jnp.einsum('bdn,bn->bd', h, C_t)
                return (h, y)
            h0 = jnp.zeros((B, D_INNER, D_STATE), dA.dtype)
            _, ys = jax.lax.scan(step, h0, (jnp.swapaxes(dA, 0, 1), jnp.swapaxes(dBu, 0, 1), jnp.swapaxes(Cm, 0, 1)))
            y = jnp.swapaxes(ys, 0, 1) + u * D
            y = y * jax.nn.silu(z)
            return jnp.einsum('bld,ed->ble', y, out_w)
        res = x
        mu = jnp.mean(x, axis=-1, keepdims=True)
        var = jnp.mean(jnp.square(x - mu), axis=-1, keepdims=True)
        xn = (x - mu) * jax.lax.rsqrt(var + 1e-05) * gamma + beta
        out_fwd = _mamba(xn, f_in_w, f_conv_w, f_conv_b, f_xproj_w, f_dt_w, f_dt_b, f_A_log, f_D, f_out_w)
        out_bwd = _mamba(xn[:, ::-1, :], b_in_w, b_conv_w, b_conv_b, b_xproj_w, b_dt_w, b_dt_b, b_A_log, b_D, b_out_w)[:, ::-1, :]
        return res + out_fwd + out_bwd

    def _L0_ffn_ref(x, Wg, bg, W0, b0, W1, b1, W2, b2):
        import jax, jax.numpy as jnp
        import numpy as np
        NUM_EXPERTS = 8
        TOP_K = 2
        D_MODEL = 128
        D_HID = 512
        BATCH, SEQ = (2, 256)
        n, s, d = x.shape
        gate_logits = x @ Wg + bg
        top_vals, top_idx = jax.lax.top_k(gate_logits, TOP_K)
        w = jax.nn.softmax(top_vals, axis=-1)
        combine = jnp.sum(jax.nn.one_hot(top_idx, NUM_EXPERTS, dtype=x.dtype) * w[..., None], axis=-2)
        xf = x.reshape(n * s, d)
        h = jnp.einsum('td,edh->eth', xf, W0) + b0[:, None, :]
        g = jax.nn.silu(jnp.einsum('td,edh->eth', xf, W1) + b1[:, None, :])
        y = jnp.einsum('eth,ehd->etd', h * g, W2) + b2[:, None, :]
        out = jnp.einsum('te,etd->td', combine.reshape(n * s, NUM_EXPERTS), y)
        return out.reshape(n, s, d)
    x = L0_attn_x
    x = _layernorm(x + _L0_attn_ref(x, L0_attn_gamma, L0_attn_beta, L0_attn_f_in_w, L0_attn_f_conv_w, L0_attn_f_conv_b, L0_attn_f_xproj_w, L0_attn_f_dt_w, L0_attn_f_dt_b, L0_attn_f_A_log, L0_attn_f_D, L0_attn_f_out_w, L0_attn_b_in_w, L0_attn_b_conv_w, L0_attn_b_conv_b, L0_attn_b_xproj_w, L0_attn_b_dt_w, L0_attn_b_dt_b, L0_attn_b_A_log, L0_attn_b_D, L0_attn_b_out_w), axis=-1)
    x = _layernorm(x + _L0_ffn_ref(x, L0_ffn_Wg, L0_ffn_bg, L0_ffn_W0, L0_ffn_b0, L0_ffn_W1, L0_ffn_b1, L0_ffn_W2, L0_ffn_b2), axis=-1)
    return x

_drawn_inputs = setup_inputs


def setup_inputs(seed=0):
    import zlib

    import numpy as np

    out = dict(_drawn_inputs(seed))
    spreads = {'L0_attn_gamma': (1.0, 0.2),
     'L0_attn_beta': (0.0, 0.1),
     'L0_attn_f_D': (1.0, 0.2),
     'L0_attn_b_D': (1.0, 0.2),
     'L0_ffn_bg': (0.0, 0.1),
     'L0_ffn_b0': (0.0, 0.8),
     'L0_ffn_b1': (0.0, 0.8),
     'L0_ffn_b2': (0.0, 0.374)}
    factors = {'L0_attn_f_conv_b': 4.893,
     'L0_attn_f_dt_b': 8.0,
     'L0_attn_b_conv_b': 5.407,
     'L0_attn_b_dt_b': 8.0,
     'L0_ffn_W0': 6.192,
     'L0_ffn_W1': 6.248,
     'L0_ffn_W2': 5.651}
    for name, (base, spread) in spreads.items():
        noise = np.random.default_rng([zlib.crc32(name.encode()), seed]).standard_normal(out[name].shape)
        drawn = base * np.exp(spread * noise) if base else spread * noise
        out[name] = jnp.asarray(drawn.astype(out[name].dtype))
    for name, factor in factors.items():
        out[name] = (out[name] * factor).astype(out[name].dtype)
    return out
```

```python
from contextlib import ExitStack

import concourse.bass as bass
import numpy as np
from concourse import mybir

F32 = mybir.dt.float32
BF16 = mybir.dt.bfloat16
ALU = mybir.AluOpType
ACT = mybir.ActivationFunctionType
AX_X = mybir.AxisListType.X
EXP_LN_TABLES = "natural_log_exp_and_others"

B, L, D = 8, 1024, 128
P = 128
DI = 2 * D
NH = DI // P
N = 16
TAPS = 4
R = 8
CH = 512
NC = L // CH
BLK = L // P
CB = CH // P
NSEG = 2 * NC
STEPS = NSEG * N
E = 8
HID = 512
HB = HID // P
UNITS = NC * E
SUBS = UNITS * HB
EPS = 1e-5
NEG = -3.0e38
BC = 2 * N
XR = 3 * BC + R
DIRS = ("f_", "b_")

PREPARE = {0: "u", 1: "conv", 5: "z", 7: "xdbl", 8: "split", 10: "dt", 11: "dtu"}
FINISH = {2: "gate", 3: "turn", 4: "out", 5: "residual"}
SLOTS = range(-2, STEPS + 6)


def pieces(k):
    found = []
    s, local = divmod(k, N)
    if k >= 0 and local in FINISH and s >= 1:
        found.append((FINISH[local], s - 1))
    if k >= 0 and local in PREPARE and s + 1 < NSEG:
        found.append((PREPARE[local], s + 1))
    return found


def scratch_tiles():
    tiles_of = {
        "u": ["u0", "u1"], "z": ["z0", "z1"], "xdbl": ["xdbl"], "dt": ["dt0", "dt1"],
        "turn": ["turn0", "turn1"], "out": ["out"],
    }
    order = [("xnT", d * NC + g) for d in range(2) for g in range(NC)]
    for name in PREPARE.values():
        order += [(t, 0) for t in tiles_of.get(name, [])]
    for k in SLOTS:
        if 0 <= k + 2 < STEPS:
            order.append(("C", k + 2))
        for name, s in pieces(k):
            order += [(t, s) for t in tiles_of.get(name, [])]
    order += [("x1T", 0), ("x1T", 1), ("logits", 0), ("combT", 0), ("combT", 1), ("b2", 0), ("b2", 1)]
    return order


SCRATCH = scratch_tiles()
SCRATCH_AT = {t: i for i, t in enumerate(SCRATCH)}
N_SCRATCH = len(SCRATCH)


def ffn_tiles():
    order = []
    for q in range(UNITS + 1):
        if q < UNITS:
            order += [("g", HB * q + j) for j in range(HB)]
        if q >= 1:
            order += [("h", HB * (q - 1) + j) for j in range(HB)]
    return order


FFN = ffn_tiles()
FFN_AT = {t: i for i, t in enumerate(FFN)}

CHAIN_M = 42
CHAIN_F = 7


def build(nc, a, out):
    x_rows = a["x"].rearrange("b (c p) d -> b p c d", p=P)
    out_rows = out.rearrange("b (c p) d -> b p c d", p=P)

    with ExitStack() as ctx:
        def sb(name, shape, dt=F32):
            return ctx.enter_context(nc.sbuf_tensor(name, shape, dt))

        def psum(name, shape, dt=F32):
            return ctx.enter_context(nc.psum_tensor(name, shape, dt))

        def sem(name):
            return ctx.enter_context(nc.semaphore(name))

        ident = sb("ident", [P, P])
        flip = sb("flip", [P, P])
        pick = sb("pick", [3 * BC, BC, P], BF16)
        prio = sb("prio", [P, E])
        in_w = sb("in_w", [P, 2, 2 * DI])
        conv_w = sb("conv_w", [P, 2, NH, TAPS])
        conv_b = sb("conv_b", [P, 2, NH])
        xproj = sb("xproj", [P, 2, NH, XR])
        dt_w = sb("dt_w", [XR, 2, DI])
        dt_b = sb("dt_b", [P, 2, NH])
        a_log = sb("a_log", [P, 2, NH, N])
        a_exp = sb("a_exp", [P, 2, NH, N])
        a_neg = sb("a_neg", [P, 2, NH, N])
        d_skip = sb("d_skip", [P, 2, NH])
        out_w = sb("out_w", [P, 2, NH, D])
        gamma = sb("gamma", [P, 1])
        beta = sb("beta", [P, 1])
        wg = sb("wg", [P, E])
        bg = sb("bg", [P, E])
        w0 = sb("w0", [P, E, HID])
        w1 = sb("w1", [P, E, HID])
        w2 = sb("w2", [P, E, HB, D])
        b0 = sb("b0", [P, E, HB])
        b1 = sb("b1", [P, E, HB])
        b2 = sb("b2", [E, D])

        x_in = sb("x_in", [P, BLK, D])
        xn = sb("xn", [P, BLK, D])
        res = sb("res", [P, BLK, D])
        stats = sb("stats", [P, BLK, 6])
        mean = sb("mean", [P, BLK])
        apart = sb("apart", [P, BLK])
        rstd = sb("rstd", [P, BLK])
        var = sb("var", [P, BLK])
        newton = sb("newton", [P, BLK])
        xnT = sb("xnT", [P, 2, L])
        u_pad = sb("u_pad", [P, NH, TAPS - 1 + L])
        uc = sb("uc", [P, NH, CH])
        gate = sb("gate", [P, 2, CB, DI])
        parts = sb("parts", [3 * BC, 2, CH], BF16)
        rest = sb("rest", [XR, CH])
        rest1, dt_low = rest[0:3 * BC, :], rest
        mid = sb("mid", [3 * BC, CH], BF16)
        dt = sb("dt", [P, 2, NH, CH])
        dtu = sb("dtu", [P, 2, NH, CH])
        du = sb("du", [P, NH, CH])
        decay = sb("decay", [P, 3, NH, CH])
        c_rep = sb("c_rep", [P, 4, CH])
        drive = sb("drive", [P, 2, NH, CH])
        state = sb("state", [P, 4, NH, CH])
        last = sb("last", [P, N, NH])
        one = sb("one", [P, NH])
        y_turn = du

        x1 = sb("x1", [P, BLK, D])
        x1T = sb("x1T", [P, L])
        logits = sb("logits", [P, BLK, E])
        work = sb("work", [P, BLK, E])
        first = sb("first", [P, BLK, E])
        second = sb("second", [P, BLK, E])
        comb = sb("comb", [P, BLK, E])
        m1 = sb("m1", [P, BLK])
        m2 = sb("m2", [P, BLK])
        vmax = sb("vmax", [P, BLK])
        gap = sb("gap", [P, BLK])
        ratio = sb("ratio", [P, BLK])
        wsum = sb("wsum", [P, BLK])
        weight1 = sb("weight1", [P, BLK])
        weight2 = sb("weight2", [P, BLK])
        combT = uc[0:E].rearrange("e h t -> e (h t)")
        g_act = sb("g_act", [P, 2, HB, CH])
        hg = sb("hg", [P, 2, CH])

        b_rep = psum("b_rep", [P, 2, CH])
        scratch = psum("scratch", [P, CH])
        y_acc = psum("y_acc", [P, CB, DI])
        ffn_in = psum("ffn_in", [P, 2, CH])
        ffn_out = psum("ffn_out", [P, CB, D])

        mamba_loaded, ffn_loaded = sem("mamba_loaded"), sem("ffn_loaded")
        x_loaded, x_used, rows_ready, stored = (sem(n) for n in ("x_loaded", "x_used", "rows_ready", "stored"))
        a_ready, one_ready, pad_ready = sem("a_ready"), sem("one_ready"), sem("pad_ready")
        var_m, root_m, log_m = sem("var_m"), sem("root_m"), sem("log_m")
        var_f, root_f, log_f = sem("var_f"), sem("root_f"), sem("log_f")
        scratch_ready, scratch_free = sem("scratch_ready"), sem("scratch_free")
        chain_m, chain_f = sem("chain_m"), sem("chain_f")
        xn_ready, conv_ready, uc_ready = sem("xn_ready"), sem("conv_ready"), sem("uc_ready")
        hi_ready, mid_ready, parts_ready = sem("hi_ready"), sem("mid_ready"), sem("parts_ready")
        exp_ready, soft_ready, dt_ready = sem("exp_ready"), sem("soft_ready"), sem("dt_ready")
        dtu_ready, du_ready = sem("dtu_ready"), sem("du_ready")
        b_ready, decay_ready, drive_ready = sem("b_ready"), sem("decay_ready"), sem("drive_ready")
        last_ready = sem("last_ready")
        scan_ready, ch_ready, summed, gated = sem("scan_ready"), sem("ch_ready"), sem("summed"), sem("gated")
        x1_ready, gap_ready, ratio_ready, comb_ready = (
            sem(n) for n in ("x1_ready", "gap_ready", "ratio_ready", "comb_ready"))
        tile_ready, g_ready, hg_ready, hg_used, unit_added = (
            sem(n) for n in ("tile_ready", "g_ready", "hg_ready", "hg_used", "unit_added"))

        def wait(eng, s, value):
            if not (isinstance(value, int) and value <= 0):
                eng.wait_ge(s, value)

        def tile_wait(eng, b, tile):
            wait(eng, scratch_ready, b * N_SCRATCH + SCRATCH_AT[tile] + 1)

        def last_count(b, k):
            s, n = divmod(k, N)
            d, c = divmod(s, NC)
            return b * 2 * (NC - 1) * N + (d * (NC - 1) + c) * N + n + 1

        def left_wait(eng, b, tile):
            wait(eng, scratch_free, b * N_SCRATCH + SCRATCH_AT[tile] + 1)

        mamba_loads = [
            (ident[:], a["ident"]), (flip[:], a["flip"]), (pick[:], a["pick"]), (prio[:], a["prio"]),
            (gamma[:], a["gamma"].rearrange("(p o) -> p o", o=1)), (beta[:], a["beta"].rearrange("(p o) -> p o", o=1)),
        ]
        for i, d in enumerate(DIRS):
            mamba_loads += [
                (in_w[:, i, :], a[d + "in_w"]),
                (conv_w[:, i], a[d + "conv_w"].rearrange("(h p) t -> p h t", p=P)),
                (conv_b[:, i], a[d + "conv_b"]),
                (dt_w[3 * BC:XR, i, :], a[d + "dt_w"]),
                (dt_b[:, i], a[d + "dt_b"]),
                (a_log[:, i], a[d + "A_log"].rearrange("(h p) n -> p h n", p=P)),
                (d_skip[:, i], a[d + "D"]),
                (out_w[:, i], a[d + "out_w"].rearrange("(h p) d -> p h d", p=P)),
                (xproj[:, i, :, 3 * BC:XR], a[d + "xproj_w"][:, 0:R].rearrange("(h p) r -> p h r", p=P)),
            ]
            for c in range(3):
                mamba_loads.append((xproj[:, i, :, c * BC:(c + 1) * BC],
                                    a[d + "xproj_w"][:, R:R + BC].rearrange("(h p) r -> p h r", p=P)))
        ffn_loads = [
            (wg[:], a["Wg"]), (bg[:], a["bg"].rearrange("(o e) -> o e", o=1).to_broadcast([P, E])),
            (w0[:], a["W0"].rearrange("e d h -> d e h")), (w1[:], a["W1"].rearrange("e d h -> d e h")),
            (w2[:], a["W2"].rearrange("e (j p) d -> p e j d", p=P)),
            (b0[:], a["b0"]), (b1[:], a["b1"]),
            (b2[:], a["b2"]),
        ]

        block = ctx.enter_context(nc.Block())

        @block.sync
        def _(sp):
            sp.sem_inc(stored, 16)
            sp.dma_start(x_in[:], x_rows[0]).then_inc(x_loaded, 16)
            for dst, src in mamba_loads:
                sp.dma_start(dst, src).then_inc(mamba_loaded, 16)
            for dst, src in ffn_loads:
                sp.dma_start(dst, src).then_inc(ffn_loaded, 16)
            for b in range(1, B + 1):
                if b < B:
                    sp.wait_ge(x_used, b)
                    sp.dma_start(x_in[:], x_rows[b]).then_inc(x_loaded, 16)
                sp.wait_ge(rows_ready, b)
                sp.dma_start(out_rows[b - 1], xn[:]).then_inc(stored, 16)
            sp.wait_ge(stored, 16 * (B + 1))

        @block.tensor
        def _(pe):
            def tile(b, name, i):
                wait(pe, scratch_free, b * N_SCRATCH + SCRATCH_AT[(name, i)])

            def xn_turn(b):
                wait(pe, xn_ready, b + 1)
                for d in range(2):
                    for g in range(NC):
                        tile(b, "xnT", d * NC + g)
                        for i in range(CB):
                            r = g * CB + i
                            mm = pe.transpose(scratch[:, i * P:(i + 1) * P], xn[:, (BLK - 1 - r) if d else r, :],
                                              (flip if d else ident)[:])
                        mm.then_inc(scratch_ready, 1)

            def piece(b, name, s):
                d, c = divmod(s, NC)
                if name == "u":
                    left_wait(pe, b, ("xnT", d * NC + c))
                    for h in range(NH):
                        tile(b, f"u{h}", s)
                        pe.matmul(scratch[:], in_w[:, d, h * P:(h + 1) * P], xnT[:, d, c * CH:(c + 1) * CH],
                                  start=True, stop=True).then_inc(scratch_ready, 1)
                elif name == "z":
                    for g in range(2):
                        tile(b, f"z{g}", s)
                        for i in range(2):
                            t0 = c * CH + (2 * g + i) * P
                            mm = pe.matmul(scratch[:, i * DI:(i + 1) * DI], xnT[:, d, t0:t0 + P],
                                           in_w[:, d, DI:2 * DI], start=True, stop=True)
                        mm.then_inc(scratch_ready, 1)
                elif name == "xdbl":
                    wait(pe, uc_ready, b * NSEG + s + 1)
                    tile(b, "xdbl", s)
                    for h in range(NH):
                        mm = pe.matmul(scratch[0:XR, :], xproj[:, d, h, :], uc[:, h, :], start=(h == 0),
                                       stop=(h == NH - 1))
                    mm.then_inc(scratch_ready, 1)
                elif name == "dt":
                    wait(pe, hi_ready, b * NSEG + s + 1)
                    for h in range(NH):
                        tile(b, f"dt{h}", s)
                        pe.matmul(scratch[:], dt_w[3 * BC:XR, d, h * P:(h + 1) * P], dt_low[3 * BC:XR, :],
                                  start=True, stop=True).then_inc(scratch_ready, 1)
                elif name == "turn":
                    wait(pe, gated, b * NSEG + s + 1)
                    for h in range(NH):
                        tile(b, f"turn{h}", s)
                        for i in range(CB):
                            at = CB - 1 - i if d else i
                            mm = pe.transpose(scratch[:, at * P:(at + 1) * P],
                                              gate[:, s % 2, i, h * P:(h + 1) * P], (flip if d else ident)[:])
                        mm.then_inc(scratch_ready, 1)
                elif name == "out":
                    left_wait(pe, b, ("turn1", s))
                    tile(b, "out", s)
                    for i in range(CB):
                        for h in range(NH):
                            mm = pe.matmul(scratch[:, i * D:(i + 1) * D], y_turn[:, h, i * P:(i + 1) * P],
                                           out_w[:, d, h, :], start=(h == 0), stop=(h == NH - 1))
                    mm.then_inc(scratch_ready, 1)

            def replicate(b, k):
                s, n = divmod(k, N)
                if n == 0:
                    wait(pe, parts_ready, b * NSEG + s + 1)
                wait(pe, drive_ready, b * STEPS + k - 1)
                pe.matmul(b_rep[:, k % 2, :], pick[:, n, :], parts[:, s % 2, :],
                          start=True, stop=True).then_inc(b_ready, 1)
                tile(b, "C", k)
                pe.matmul(scratch[:], pick[:, N + n, :], parts[:, s % 2, :],
                          start=True, stop=True).then_inc(scratch_ready, 1)

            def sum_states(b, k):
                s, n = divmod(k, N)
                if n == 0:
                    wait(pe, gated, b * NSEG + s)
                    wait(pe, du_ready, b * NSEG + s + 1)
                    for i in range(CB):
                        for h in range(NH):
                            pe.matmul(y_acc[:, i, h * P:(h + 1) * P], du[:, h, i * P:(i + 1) * P], ident[:],
                                      start=(i % 2 == 0 and h == 0), stop=False, is_transpose=True,
                                      skip_group_check=True)
                wait(pe, ch_ready, b * STEPS + k + 1)
                for i in range(CB):
                    for h in range(NH):
                        mm = pe.matmul(y_acc[:, i, h * P:(h + 1) * P], state[:, k % 4, h, i * P:(i + 1) * P],
                                       ident[:], start=False, stop=(n == N - 1), is_transpose=True,
                                       skip_group_check=True)
                mm.then_inc(summed, 1)

            def ffn_tile(fb, kind, sub):
                at = FFN_AT[(kind, sub)]
                if at >= 2:
                    old = FFN[at - 2]
                    wait(pe, g_ready if old[0] == "g" else hg_ready, fb * SUBS + old[1] + 1)
                u, j = divmod(sub, HB)
                c, e = divmod(u, E)
                pe.matmul(ffn_in[:, at % 2, :], (w1 if kind == "g" else w0)[:, e, j * P:(j + 1) * P],
                          x1T[:, c * CH:(c + 1) * CH], start=True, stop=True).then_inc(tile_ready, 1)

            def ffn_down(fb, sub):
                u, j = divmod(sub, HB)
                e = u % E
                wait(pe, hg_ready, fb * SUBS + sub + 1)
                if j == 0 and u:
                    wait(pe, unit_added, fb * UNITS + u)
                for i in range(CB):
                    mm = pe.matmul(ffn_out[:, i, :], hg[:, sub % 2, i * P:(i + 1) * P], w2[:, e, j, :],
                                   start=(j == 0 and i == 0), stop=(j == HB - 1), skip_group_check=True)
                mm.then_inc(hg_used, 1)

            def ffn_slot(fb, k):
                if k < 0 or k > SUBS + HB:
                    return
                if k % HB == 0 and k < SUBS:
                    for j in range(HB):
                        ffn_tile(fb, "g", k + j)
                if HB <= k < SUBS + HB:
                    ffn_tile(fb, "h", k - HB)
                if HB < k:
                    ffn_down(fb, k - HB - 1)

            def route(b):
                wait(pe, x1_ready, b + 1)
                for g in range(NC):
                    tile(b, "x1T", g)
                    for i in range(CB):
                        mm = pe.transpose(scratch[:, i * P:(i + 1) * P], x1[:, g * CB + i, :], ident[:])
                    mm.then_inc(scratch_ready, 1)
                left_wait(pe, b, ("x1T", NC - 1))
                tile(b, "logits", 0)
                for i in range(BLK):
                    mm = pe.matmul(scratch[:, i * E:(i + 1) * E], x1T[:, i * P:(i + 1) * P], wg[:],
                                   start=True, stop=True)
                mm.then_inc(scratch_ready, 1)
                wait(pe, comb_ready, b + 1)
                for g in range(NC):
                    tile(b, "combT", g)
                    for i in range(CB):
                        mm = pe.matmul(scratch[0:E, i * P:(i + 1) * P], comb[:, g * CB + i, :], ident[:],
                                       start=True, stop=True)
                    mm.then_inc(scratch_ready, 1)
                left_wait(pe, b, ("combT", NC - 1))
                for g in range(NC):
                    tile(b, "b2", g)
                    for i in range(CB):
                        mm = pe.matmul(scratch[:, i * D:(i + 1) * D], combT[:, (g * CB + i) * P:(g * CB + i + 1) * P],
                                       b2[:], start=True, stop=True)
                    mm.then_inc(scratch_ready, 1)

            def sequence(b, mamba, ffn):
                if mamba:
                    xn_turn(b)
                    for name in PREPARE.values():
                        piece(b, name, 0)
                for k in SLOTS:
                    if mamba:
                        if 0 <= k + 2 < STEPS:
                            replicate(b, k + 2)
                        for name, s in pieces(k):
                            piece(b, name, s)
                        if 0 <= k - 2 < STEPS:
                            sum_states(b, k - 2)
                    if ffn:
                        ffn_slot(b - 1, k)
                if mamba:
                    route(b)

            pe.wait_ge(mamba_loaded, 16 * len(mamba_loads))
            sequence(0, True, False)
            pe.wait_ge(ffn_loaded, 16 * len(ffn_loads))
            with pe.Fori(1, B) as b:
                sequence(b, True, True)
            sequence(B, False, True)

        @block.scalar
        def _(act):
            def exp_ln_tables():
                act.preload_act_table_set(EXP_LN_TABLES)

            def norm_root(of_mamba, nth):
                got, log, root = (var_m, log_m, root_m) if of_mamba else (var_f, log_f, root_f)
                wait(act, got, nth + 1)
                act.activation(rstd[:], var[:], ACT.Ln).then_inc(log, 1)
                wait(act, log, nth + 1)
                act.activation(rstd[:], rstd[:], ACT.Exp, scale=-0.5).then_inc(root, 1)

            def xn_turn(b):
                norm_root(True, 2 * b)
                for d in range(2):
                    for g in range(NC):
                        tile_wait(act, b, ("xnT", d * NC + g))
                        act.activation(xnT[:, d, g * CH:(g + 1) * CH], scratch[:], ACT.Identity, bias=beta[:],
                                       scale=gamma[:]).then_inc(scratch_free, 1)

            def piece(b, name, s):
                d, c = divmod(s, NC)
                if name == "u":
                    wait(act, conv_ready, b * NSEG + s)
                    for h in range(NH):
                        tile_wait(act, b, (f"u{h}", s))
                        t0 = TAPS - 1 + c * CH
                        act.activation(u_pad[:, h, t0:t0 + CH], scratch[:], ACT.Copy).then_inc(scratch_free, 1)
                elif name == "z":
                    for g in range(2):
                        tile_wait(act, b, (f"z{g}", s))
                        act.activation(gate[:, s % 2, 2 * g:2 * g + 2, :],
                                       scratch[:].rearrange("p (i e) -> p i e", i=2), ACT.Silu).then_inc(scratch_free, 1)
                    wait(act, conv_ready, b * NSEG + s + 1)
                    act.activation(uc[:], uc[:], ACT.Silu).then_inc(uc_ready, 1)
                    exp_ln_tables()
                elif name == "xdbl":
                    tile_wait(act, b, ("xdbl", s))
                    act.activation(parts[:, s % 2, :], scratch[0:3 * BC, :], ACT.Copy)
                    act.activation(dt_low[3 * BC:XR, :], scratch[3 * BC:XR, :], ACT.Copy).then_inc(hi_ready, 1)
                elif name == "split":
                    left_wait(act, b, ("xdbl", s))
                    act.activation(parts[BC:2 * BC, s % 2, :], rest1[BC:2 * BC, :], ACT.Copy)
                    act.activation(mid[2 * BC:, :], rest1[2 * BC:, :], ACT.Copy).then_inc(mid_ready, 1)
                elif name == "dt":
                    wait(act, drive_ready, b * STEPS + N * (s - 1))
                    for h in range(NH):
                        tile_wait(act, b, (f"dt{h}", s))
                        act.activation(dtu[:, s % 2, h, :], scratch[:], ACT.Identity, bias=dt_b[:, d, h:h + 1])
                        act.activation(dt[:, s % 2, h, :], scratch[:], ACT.Abs,
                                       bias=dt_b[:, d, h:h + 1]).then_inc(scratch_free, 1)
                    left_wait(act, b, ("dt1", s))
                    act.activation(dt[:, s % 2], dt[:, s % 2], ACT.Exp, scale=-1.0).then_inc(exp_ready, 1)
                    wait(act, exp_ready, b * NSEG + s + 1)
                    act.activation(dt[:, s % 2], dt[:, s % 2], ACT.Ln, bias=1.0).then_inc(soft_ready, 1)
                elif name == "turn":
                    for h in range(NH):
                        tile_wait(act, b, (f"turn{h}", s))
                        act.activation(y_turn[:, h, :], scratch[:], ACT.Copy).then_inc(scratch_free, 1)

            def step_ahead(b, k):
                wait(act, ch_ready, b * STEPS + k - 3)
                tile_wait(act, b, ("C", k))
                act.activation(c_rep[:, k % 4, :], scratch[:], ACT.Copy).then_inc(scratch_free, 1)

            def decays(b, k):
                s, n = divmod(k, N)
                d = s // NC
                if n == 0:
                    wait(act, dt_ready, b * NSEG + s + 1)
                wait(act, scan_ready, b * STEPS + k - 2)
                for h in range(NH):
                    e = act.activation(decay[:, k % 3, h, :], dt[:, s % 2, h, :], ACT.Exp,
                                       scale=a_neg[:, d, h, n:n + 1])
                e.then_inc(decay_ready, 1)

            def ffn_slot(fb, k):
                if k < 0 or k >= SUBS or k % HB:
                    return
                u = k // HB
                if u >= 2:
                    wait(act, hg_ready, fb * SUBS + (u - 1) * HB)
                for j in range(HB):
                    wait(act, tile_ready, fb * 2 * SUBS + FFN_AT[("g", k + j)] + 1)
                    act.activation(g_act[:, u % 2, j, :], ffn_in[:, FFN_AT[("g", k + j)] % 2, :], ACT.Silu,
                                   bias=b1[:, u % E, j:j + 1]).then_inc(g_ready, 1)
                exp_ln_tables()

            def route(b):
                for g in range(NC):
                    tile_wait(act, b, ("x1T", g))
                    act.activation(x1T[:, g * CH:(g + 1) * CH], scratch[:], ACT.Copy).then_inc(scratch_free, 1)
                wait(act, gap_ready, b + 1)
                act.activation(ratio[:], gap[:], ACT.Exp).then_inc(ratio_ready, 1)
                for g in range(NC):
                    tile_wait(act, b, ("combT", g))
                    act.activation(combT[:, g * CH:(g + 1) * CH], scratch[0:E, :], ACT.Copy).then_inc(scratch_free, 1)

            def sequence(b, mamba, ffn):
                if mamba:
                    xn_turn(b)
                    for name in PREPARE.values():
                        piece(b, name, 0)
                for k in SLOTS:
                    if mamba:
                        if 0 <= k + 2 < STEPS:
                            step_ahead(b, k + 2)
                        for name, s in pieces(k):
                            piece(b, name, s)
                        if 0 <= k + 2 < STEPS:
                            decays(b, k + 2)
                    if ffn:
                        ffn_slot(b - 1, k)
                if ffn:
                    norm_root(False, b - 1)
                if mamba:
                    norm_root(True, 2 * b + 1)
                    route(b)

            act.wait_ge(mamba_loaded, 16 * len(mamba_loads))
            exp_ln_tables()
            act.activation(a_exp[:], a_log[:], ACT.Exp).then_inc(a_ready, 1)
            act.wait_ge(a_ready, 1)
            act.activation(a_neg[:], a_exp[:], ACT.Copy, scale=-1.0).then_inc(a_ready, 1)
            act.wait_ge(a_ready, 2)
            sequence(0, True, False)
            act.wait_ge(ffn_loaded, 16 * len(ffn_loads))
            with act.Fori(1, B) as b:
                sequence(b, True, True)
            sequence(B, False, True)

        @block.gpsimd
        def _(pool):
            def sequence(b):
                for k in range(STEPS):
                    s, n = divmod(k, N)
                    pool.wait_ge(scan_ready, b * STEPS + k + 1)
                    left_wait(pool, b, ("C", k))
                    if s % NC < NC - 1:
                        pool.tensor_tensor(last[:, n, :], state[:, k % 4, :, CH - 1], one[:],
                                           ALU.mult).then_inc(last_ready, 1)
                        pool.wait_ge(last_ready, last_count(b, k))
                    pool.tensor_tensor(state[:, k % 4], state[:, k % 4],
                                       c_rep[:, k % 4:k % 4 + 1, :].to_broadcast([P, NH, CH]),
                                       ALU.mult).then_inc(ch_ready, 1)

            pool.memset(one[:], 1.0).then_inc(one_ready, 1)
            pool.wait_ge(one_ready, 1)
            with pool.Fori(0, B) as b:
                sequence(b)

        @block.vector
        def _(dve):
            chained = {"m": 0, "f": 0}

            def link(b, ins, which="m"):
                chained[which] += 1
                s, per = (chain_m, CHAIN_M) if which == "m" else (chain_f, CHAIN_F)
                ins.then_inc(s, 1)
                dve.wait_ge(s, b * per + chained[which])

            def layer_norm(b, dst, src, which, nth):
                for i in range(BLK):
                    ins = dve.bn_stats(stats[:, i, :], src[:, i, :])
                link(b, ins, which)
                dve.tensor_tensor(mean[:], stats[:, :, 1], stats[:, :, 4], ALU.add)
                dve.tensor_tensor(apart[:], stats[:, :, 1], stats[:, :, 4], ALU.subtract)
                link(b, dve.tensor_tensor(var[:], stats[:, :, 2], stats[:, :, 5], ALU.add), which)
                dve.tensor_scalar(mean[:], mean[:], 0.5, None, ALU.mult)
                dve.tensor_scalar(var[:], var[:], 1.0 / D, EPS, ALU.mult, ALU.add)
                link(b, dve.scalar_tensor_tensor(apart[:], apart[:], 0.25, apart[:], ALU.mult, ALU.mult), which)
                dve.tensor_tensor(var[:], var[:], apart[:], ALU.add).then_inc(
                    var_m if which == "m" else var_f, 1)
                wait(dve, root_m if which == "m" else root_f, nth + 1)
                link(b, dve.tensor_tensor(newton[:], var[:], rstd[:], ALU.mult), which)
                link(b, dve.tensor_tensor(newton[:], newton[:], rstd[:], ALU.mult), which)
                link(b, dve.tensor_scalar(newton[:], newton[:], -0.5, 1.5, ALU.mult, ALU.add), which)
                link(b, dve.tensor_tensor(rstd[:], rstd[:], newton[:], ALU.mult), which)
                for i in range(BLK):
                    ins = dve.tensor_scalar(dst[:, i, :], src[:, i, :], mean[:, i:i + 1], rstd[:, i:i + 1],
                                            ALU.subtract, ALU.mult)
                return ins

            def first_norm(b):
                dve.wait_ge(x_loaded, 16 * (b + 1))
                wait(dve, stored, 16 * b)
                layer_norm(b, xn, x_in, "m", 2 * b).then_inc(xn_ready, 1)
                dve.tensor_scalar(res[:], x_in[:], 2.0, None, ALU.mult).then_inc(x_used, 1)

            def piece(b, name, s):
                d, c = divmod(s, NC)
                if name == "conv":
                    left_wait(dve, b, ("u1", s))
                    for t in reversed(range(TAPS)):
                        for h in range(NH):
                            taps = u_pad[:, h, c * CH + t:c * CH + t + CH]
                            w = conv_w[:, d, h, t:t + 1]
                            if t == TAPS - 1:
                                ins = dve.tensor_scalar(uc[:, h, :], taps, w, conv_b[:, d, h:h + 1], ALU.mult, ALU.add)
                            else:
                                ins = dve.scalar_tensor_tensor(uc[:, h, :], taps, w, uc[:, h, :], ALU.mult, ALU.add)
                        if t:
                            link(b, ins)
                    ins.then_inc(conv_ready, 1)
                elif name == "xdbl":
                    wait(dve, hi_ready, b * NSEG + s + 1)
                    dve.tensor_tensor(rest1, scratch[0:3 * BC, :], parts[:, s % 2, :],
                                      ALU.subtract).then_inc(scratch_free, 1)
                elif name == "split":
                    wait(dve, mid_ready, b * NSEG + s + 1)
                    dve.tensor_tensor(parts[2 * BC:, s % 2, :], rest1[2 * BC:, :], mid[2 * BC:, :],
                                      ALU.subtract).then_inc(parts_ready, 1)
                elif name == "dtu":
                    wait(dve, soft_ready, b * NSEG + s + 1)
                    dve.scalar_tensor_tensor(dt[:, s % 2], dtu[:, s % 2], 0.0, dt[:, s % 2], ALU.max,
                                             ALU.add).then_inc(dt_ready, 1)
                    wait(dve, uc_ready, b * NSEG + s + 1)
                    wait(dve, summed, b * STEPS + N * (s - 1) + 1)
                    for h in range(NH):
                        ins = dve.tensor_scalar(du[:, h, :], uc[:, h, :], d_skip[:, d, h:h + 1], None, ALU.mult)
                    ins.then_inc(du_ready, 1)
                    wait(dve, dt_ready, b * NSEG + s + 1)
                    dve.tensor_tensor(dtu[:, s % 2], dt[:, s % 2], uc[:], ALU.mult).then_inc(dtu_ready, 1)
                elif name == "gate":
                    wait(dve, summed, b * STEPS + N * (s + 1))
                    left_wait(dve, b, ("z1", s))
                    for g in range(2):
                        ins = dve.tensor_tensor(gate[:, s % 2, 2 * g:2 * g + 2, :], y_acc[:, 2 * g:2 * g + 2, :],
                                                gate[:, s % 2, 2 * g:2 * g + 2, :], ALU.mult)
                    ins.then_inc(gated, 1)
                elif name == "residual":
                    tile_wait(dve, b, ("out", s))
                    at = CB * (NC - 1 - c if d else c)
                    dve.tensor_tensor(res[:, at:at + CB, :], scratch[:].rearrange("p (i e) -> p i e", i=CB),
                                      res[:, at:at + CB, :], ALU.add).then_inc(scratch_free, 1)

            def drive_step(b, k):
                s, n = divmod(k, N)
                if n == 0:
                    wait(dve, dtu_ready, b * NSEG + s + 1)
                wait(dve, b_ready, b * STEPS + k + 1)
                wait(dve, scan_ready, b * STEPS + k - 1)
                dve.tensor_tensor(drive[:, k % 2], dtu[:, s % 2],
                                  b_rep[:, k % 2:k % 2 + 1, :].to_broadcast([P, NH, CH]),
                                  ALU.mult).then_inc(drive_ready, 1)

            def scan_step(b, k):
                s, n = divmod(k, N)
                wait(dve, drive_ready, b * STEPS + k + 1)
                wait(dve, decay_ready, b * STEPS + k + 1)
                wait(dve, summed, b * STEPS + k - 3)
                if s % NC:
                    wait(dve, last_ready, last_count(b, k - N))
                for h in range(NH):
                    ins = dve.tensor_tensor_scan(state[:, k % 4, h, :], decay[:, k % 3, h, :], drive[:, k % 2, h, :],
                                                 last[:, n, h:h + 1] if s % NC else 0.0, ALU.mult, ALU.add)
                ins.then_inc(scan_ready, 1)

            def add_unit(fb, u):
                c, e = divmod(u, E)
                wait(dve, hg_used, fb * SUBS + HB * (u + 1))
                if u:
                    wait(dve, unit_added, fb * UNITS + u)
                for i in range(CB):
                    r = c * CB + i
                    ins = dve.scalar_tensor_tensor(x1[:, r, :], ffn_out[:, i, :], comb[:, r, e:e + 1], x1[:, r, :],
                                                   ALU.mult, ALU.add)
                ins.then_inc(unit_added, 1)

            def ffn_slot(fb, k):
                if k > HB and (k - 1) % HB == 0 and k >= 2 * HB + 1:
                    add_unit(fb, (k - 1) // HB - 2)
                sub = k - HB
                if 0 <= sub < SUBS:
                    u, j = divmod(sub, HB)
                    at = FFN_AT[("h", sub)]
                    wait(dve, tile_ready, fb * 2 * SUBS + at + 1)
                    wait(dve, g_ready, fb * SUBS + sub + 1)
                    if sub >= 2:
                        wait(dve, hg_used, fb * SUBS + sub - 1)
                    dve.scalar_tensor_tensor(hg[:, sub % 2, :], ffn_in[:, at % 2, :], b0[:, u % E, j:j + 1],
                                             g_act[:, u % 2, j, :], ALU.add, ALU.mult).then_inc(hg_ready, 1)

            def first_best(b, of, best, mask):
                def spread(v):
                    return v[:].rearrange("p (i o) -> p i o", o=1).to_broadcast([P, BLK, E])

                link(b, dve.tensor_reduce(best[:], of[:], AX_X, ALU.max))
                link(b, dve.tensor_tensor(mask[:], of[:], spread(best), ALU.is_equal))
                link(b, dve.tensor_tensor(mask[:], mask[:], prio[:].rearrange("p (o e) -> p o e", o=1)
                                          .to_broadcast([P, BLK, E]), ALU.mult))
                link(b, dve.tensor_reduce(vmax[:], mask[:], AX_X, ALU.max))
                link(b, dve.tensor_tensor(mask[:], mask[:], spread(vmax), ALU.is_equal))

            def route(b):
                def spread(v):
                    return v[:].rearrange("p (i o) -> p i o", o=1).to_broadcast([P, BLK, E])

                left_wait(dve, b, ("out", NSEG - 1))
                layer_norm(b, x1, res, "m", 2 * b + 1).then_inc(x1_ready, 1)
                tile_wait(dve, b, ("logits", 0))
                dve.tensor_tensor(logits[:], scratch[:, 0:BLK * E].rearrange("p (i e) -> p i e", i=BLK),
                                  bg[:].rearrange("p (o e) -> p o e", o=1).to_broadcast([P, BLK, E]),
                                  ALU.add).then_inc(scratch_free, 1)
                left_wait(dve, b, ("logits", 0))
                first_best(b, logits, m1, first)
                link(b, dve.scalar_tensor_tensor(work[:], first[:], NEG, logits[:], ALU.mult, ALU.add))
                first_best(b, work, m2, second)
                dve.tensor_tensor(gap[:], m2[:], m1[:], ALU.subtract).then_inc(gap_ready, 1)
                dve.wait_ge(ratio_ready, b + 1)
                link(b, dve.tensor_scalar(wsum[:], ratio[:], 1.0, None, ALU.add))
                link(b, dve.reciprocal(weight1[:], wsum[:]))
                link(b, dve.tensor_tensor(weight2[:], weight1[:], ratio[:], ALU.mult))
                link(b, dve.tensor_tensor(first[:], first[:], spread(weight1), ALU.mult))
                link(b, dve.tensor_tensor(second[:], second[:], spread(weight2), ALU.mult))
                dve.tensor_tensor(comb[:], first[:], second[:], ALU.add).then_inc(comb_ready, 1)
                for g in range(NC):
                    tile_wait(dve, b, ("b2", g))
                    rows = x1[:, g * CB:(g + 1) * CB, :]
                    dve.tensor_tensor(rows, scratch[:].rearrange("p (i e) -> p i e", i=CB), rows,
                                      ALU.add).then_inc(scratch_free, 1)
                left_wait(dve, b, ("b2", NC - 1))

            def sequence(b, mamba, ffn):
                chained.update(m=0, f=0)
                if mamba:
                    first_norm(b)
                    for name in PREPARE.values():
                        piece(b, name, 0)
                for k in SLOTS:
                    if mamba:
                        if 0 <= k + 1 < STEPS:
                            drive_step(b, k + 1)
                        for name, s in pieces(k):
                            piece(b, name, s)
                        if 0 <= k < STEPS:
                            scan_step(b, k)
                    if ffn:
                        ffn_slot(b - 1, k)
                if ffn:
                    wait(dve, unit_added, b * UNITS)
                    wait(dve, stored, 16 * b)
                    layer_norm(b - 1, xn, x1, "f", b - 1).then_inc(rows_ready, 1)
                if mamba:
                    route(b)
                assert chained == {"m": CHAIN_M if mamba else 0, "f": CHAIN_F if ffn else 0}, chained

            dve.memset(u_pad[:, :, 0:TAPS - 1], 0.0).then_inc(pad_ready, 1)
            dve.wait_ge(pad_ready, 1)
            dve.wait_ge(mamba_loaded, 16 * len(mamba_loads))
            dve.wait_ge(ffn_loaded, 16 * len(ffn_loads))
            sequence(0, True, False)
            with dve.Fori(1, B) as b:
                sequence(b, True, True)
            sequence(B, False, True)


def kernel(**inputs):
    import numpy as _np
    import concourse.bacc as _bacc
    from concourse import mybir as _mybir
    from concourse.bass_utils import run_bass_kernel_spmd as _run

    def flat(v):
        return _np.ascontiguousarray(v)

    laid = {"x": flat(inputs["L0_attn_x"]), "gamma": flat(inputs["L0_attn_gamma"]), "beta": flat(inputs["L0_attn_beta"])}
    for d in ("f_", "b_"):
        pre = "L0_attn_" + d
        for name in ("in_w", "xproj_w", "dt_w", "out_w"):
            laid[d + name] = flat(_np.asarray(inputs[pre + name]).T)
        laid[d + "conv_w"] = flat(_np.asarray(inputs[pre + "conv_w"])[:, 0, :])
        laid[d + "A_log"] = flat(inputs[pre + "A_log"])
        for name in ("conv_b", "dt_b", "D"):
            laid[d + name] = flat(_np.asarray(inputs[pre + name]).reshape(NH, P).T)
    for name in ("Wg", "bg", "W0", "W1", "W2", "b2"):
        laid[name] = flat(inputs["L0_ffn_" + name])
    for name in ("b0", "b1"):
        laid[name] = flat(_np.asarray(inputs["L0_ffn_" + name]).reshape(E, HB, P).transpose(2, 0, 1))
    laid["ident"] = _np.eye(P, dtype=_np.float32)
    laid["flip"] = flat(_np.eye(P, dtype=_np.float32)[::-1])
    rows = _np.arange(3 * BC)[:, None, None] % BC == _np.arange(BC)[None, :, None]
    import ml_dtypes as _ml
    laid["pick"] = flat(_np.broadcast_to(rows, (3 * BC, BC, P)).astype(_ml.bfloat16))
    laid["prio"] = flat(_np.broadcast_to(_np.arange(E, 0, -1, dtype=_np.float32), (P, E)))

    nc = _bacc.Bacc("TRN2", target_bir_lowering=False, num_devices=1)
    arrays, args = {}, {}
    for name, v in laid.items():
        arrays[f"in_{name}"] = v
        args[name] = nc.dram_tensor(f"in_{name}", v.shape, _mybir.dt.from_np(v.dtype), kind="ExternalInput").ap()
    out = nc.dram_tensor("out_0", (B, L, D), F32, kind="ExternalOutput").ap()
    build(nc, args, out)
    r = _run(nc, [arrays], core_ids=[0])
    return r.results[0]["out_0"]
```

```python
from contextlib import ExitStack

import concourse.bass as bass
import numpy as np
from concourse import mybir

F32 = mybir.dt.float32
BF16 = mybir.dt.bfloat16
ALU = mybir.AluOpType
ACT = mybir.ActivationFunctionType
AX_X = mybir.AxisListType.X
EXP_LN_TABLES = "natural_log_exp_and_others"

B, L, D = 8, 1024, 128
P = 128
DI = 2 * D
NH = DI // P
N = 16
TAPS = 4
R = 8
CH = 512
NC = L // CH
BLK = L // P
CB = CH // P
NSEG = 2 * NC
STEPS = NSEG * N
E = 8
HID = 512
HB = HID // P
UNITS = NC * E
SUBS = UNITS * HB
EPS = 1e-5
NEG = -3.0e38
BC = 2 * N
XR = 3 * BC + R
DIRS = ("f_", "b_")

PREPARE = {0: ("u", 0), 1: ("u", 1), 2: ("conv", 0), 6: ("z", 0), 8: ("xdbl", 0), 9: ("split", 0),
           10: ("dt", 0), 11: ("dt", 1), 12: ("dtu", 0)}
FINISH = {2: ("gate", 0), 3: ("turn", 0), 4: ("turn", 1), 6: ("out", 0)}
NEXT_NORM = {17: ("stats", 0), 18: ("spread", 0), 20: ("normal", 0), 22: ("xnT", 0), 23: ("xnT", 1),
             41: ("xnT", 2), 42: ("xnT", 3)}
ROUTE = {7: ("stats", 1), 8: ("spread", 1), 9: ("normal", 1), 10: ("x1T", 0), 11: ("logits", 0),
         12: ("comb", 0), 13: ("combT", 0), 14: ("b2", 0)}
SECOND = {"z": 1, "x1T": 1, "combT": 1, "b2": 1}
OUT_NORM = {61: ("stats", 2), 62: ("spread", 2), 63: ("normal", 2)}
FFN_FROM = 12
UNIT_SLOTS = (0, 0, 1, 2)


def slot_events(k):
    def at(step):
        return step // STEPS, step % STEPS

    seg, local = divmod(k, N)
    later, events = [], []
    off, step = at(k + 2)
    events += [("replicate", off, step), ("decay", off, step)]
    off, step = at(k + 1)
    events += [("drive", off, step), ("scan", 0, k)]
    off, step = at(k - 2)
    events.append(("sum", off, step))
    tiles = []
    if local in FINISH:
        name, i = FINISH[local]
        tiles.append((name, (seg - 1) // NSEG, (seg - 1) % NSEG, i))
    if local in PREPARE:
        name, i = PREPARE[local]
        tiles.append((name, (seg + 1) // NSEG, (seg + 1) % NSEG, i))
    for table, off in ((NEXT_NORM, 1), (ROUTE, -1), (OUT_NORM, -1)):
        if k in table:
            tiles.append((table[k][0], off, 0, table[k][1]))
    for e in tiles:
        events.append(e)
        if e[0] in SECOND:
            later.append((e[0], e[1], e[2], 1))
    u, r = divmod(k - FFN_FROM, 3)
    if r == 2 and 0 <= u + 1 < UNITS:
        events.append(("gates", -1, u + 1))
    down, hidden = {0: ((-1, 3),), 1: ((0, 0), (0, 1)), 2: ((0, 2),)}[r], {0: (0, 1), 1: (2,), 2: (3,)}[r]
    for du, j in down:
        if 0 <= u + du < UNITS:
            events.append(("down", -1, (u + du) * HB + j))
            if j == HB - 1:
                events.append(("add", -1, u + du))
    for j in hidden:
        if 0 <= u < UNITS:
            events.append(("hidden", -1, u * HB + j))
    return events + later


ITERATION = [e for k in range(STEPS) for e in slot_events(k)]
SCRATCH_TILES = ("u", "z", "xdbl", "dt", "turn", "out", "xnT", "x1T", "logits", "combT", "b2")
LINKS = {"conv": TAPS - 1, "spread": 2, "normal": 4, "stats": 0, "logits": 11, "comb": 5}


def events_of(b):
    return [e for e in ITERATION if not isinstance(b, int) or 0 <= b + e[1] < B]


def before(b, count):
    if isinstance(b, int):
        return sum(count(i) for i in range(-1, b))
    return before(1, count) + (b - 1) * count(1)


def tiles_of(b):
    return [e for e in events_of(b) if e[0] in SCRATCH_TILES]


def norms_of(b):
    return [e for e in events_of(b) if e[0] == "spread"]


def iterations(eng, do):
    do(-1)
    do(0)
    with eng.Fori(1, B - 1) as b:
        do(b)
    do(B - 1)
    do(B)


FFN = [("g", HB * e[2] + j) if e[0] == "gates" else ("h", e[2]) for e in ITERATION
       if e[0] in ("gates", "hidden") for j in range(HB if e[0] == "gates" else 1)]
FFN_AT = {t: i for i, t in enumerate(FFN)}
assert len(FFN) == 2 * SUBS


def build(nc, a, out):
    x_rows = a["x"].rearrange("b (c p) d -> b p c d", p=P)
    out_rows = out.rearrange("b (c p) d -> b p c d", p=P)

    with ExitStack() as ctx:
        def sb(name, shape, dt=F32):
            return ctx.enter_context(nc.sbuf_tensor(name, shape, dt))

        def psum(name, shape, dt=F32):
            return ctx.enter_context(nc.psum_tensor(name, shape, dt))

        def sem(name):
            return ctx.enter_context(nc.semaphore(name))

        ident = sb("ident", [P, P])
        flip = sb("flip", [P, P])
        pick = sb("pick", [3 * BC, BC, P], BF16)
        prio = sb("prio", [P, E])
        in_w = sb("in_w", [P, 2, 2 * DI])
        conv_w = sb("conv_w", [P, 2, NH, TAPS])
        conv_b = sb("conv_b", [P, 2, NH])
        xproj = sb("xproj", [P, 2, NH, XR])
        dt_w = sb("dt_w", [XR, 2, DI])
        dt_b = sb("dt_b", [P, 2, NH])
        a_log = sb("a_log", [P, 2, NH, N])
        a_exp = sb("a_exp", [P, 2, NH, N])
        a_neg = sb("a_neg", [P, 2, NH, N])
        d_skip = sb("d_skip", [P, 2, NH])
        out_w = sb("out_w", [P, 2, NH, D])
        gamma = sb("gamma", [P, 1])
        beta = sb("beta", [P, 1])
        wg = sb("wg", [P, E])
        bg = sb("bg", [P, E])
        w0 = sb("w0", [P, E, HID])
        w1 = sb("w1", [P, E, HID])
        w2 = sb("w2", [P, E, HB, D])
        b0 = sb("b0", [P, E, HB])
        b1 = sb("b1", [P, E, HB])
        b2 = sb("b2", [E, D])

        xn = sb("xn", [P, BLK, D])
        res = sb("res", [P, BLK, D])
        stats = sb("stats", [P, BLK, 6])
        mean = sb("mean", [P, BLK])
        apart = sb("apart", [P, BLK])
        rstd = sb("rstd", [P, BLK])
        var = sb("var", [P, BLK])
        newton = sb("newton", [P, BLK])
        xnT = sb("xnT", [P, 2, L])
        u_pad = sb("u_pad", [P, NH, TAPS - 1 + L])
        uc = sb("uc", [P, NH, CH])
        gate = sb("gate", [P, 2, CB, DI])
        parts = sb("parts", [3 * BC, 2, CH], BF16)
        rest = sb("rest", [XR, CH])
        dt_low = rest
        mid = sb("mid", [3 * BC, CH], BF16)
        dt = sb("dt", [P, 2, NH, CH])
        dtu = sb("dtu", [P, 2, NH, CH])
        du = sb("du", [P, NH, CH])
        decay = sb("decay", [P, 4, NH, CH])
        c_rep = sb("c_rep", [P, 4, CH])
        drive = sb("drive", [P, 2, NH, CH])
        state = sb("state", [P, 4, NH, CH])
        last = sb("last", [P, N, NH])
        one = sb("one", [P, NH])
        y_turn = du

        x1 = sb("x1", [P, BLK, D])
        x1T = sb("x1T", [P, L])
        logits = sb("logits", [P, BLK, E])
        work = sb("work", [P, BLK, E])
        first = sb("first", [P, BLK, E])
        second = sb("second", [P, BLK, E])
        comb = sb("comb", [P, BLK, E])
        m1 = sb("m1", [P, BLK])
        m2 = sb("m2", [P, BLK])
        vmax = sb("vmax", [P, BLK])
        gap = sb("gap", [P, BLK])
        ratio = sb("ratio", [P, BLK])
        wsum = sb("wsum", [P, BLK])
        weight1 = sb("weight1", [P, BLK])
        weight2 = sb("weight2", [P, BLK])
        combT = uc[0:E].rearrange("e h t -> e (h t)")
        g_act = sb("g_act", [P, 2, HB, CH])
        hg = sb("hg", [P, 2, CH])

        b_rep = psum("b_rep", [P, 2, CH])
        scratch = psum("scratch", [P, CH])
        y_acc = psum("y_acc", [P, CB, DI])
        ffn_in = psum("ffn_in", [P, 2, CH])
        ffn_out = psum("ffn_out", [P, CB, D])

        mamba_loaded, ffn_loaded = sem("mamba_loaded"), sem("ffn_loaded")
        x_loaded, res_loaded, rows_ready, stored = (sem(n) for n in ("x_loaded", "res_loaded", "rows_ready", "stored"))
        a_ready, one_ready, pad_ready = sem("a_ready"), sem("one_ready"), sem("pad_ready")
        stats_ready, var_ready, log_ready, root_ready = sem("stats_ready"), sem("var_ready"), sem("log_ready"), sem("root_ready")
        scratch_ready, scratch_free, chain = sem("scratch_ready"), sem("scratch_free"), sem("chain")
        xn_ready, conv_ready, uc_ready = sem("xn_ready"), sem("conv_ready"), sem("uc_ready")
        hi_ready, mid_ready, parts_ready = sem("hi_ready"), sem("mid_ready"), sem("parts_ready")
        exp_ready, soft_ready, dt_ready = sem("exp_ready"), sem("soft_ready"), sem("dt_ready")
        dtu_ready, du_ready = sem("dtu_ready"), sem("du_ready")
        b_ready, c_ready, c_copied = sem("b_ready"), sem("c_ready"), sem("c_copied")
        decay_ready, drive_ready, scan_ready = sem("decay_ready"), sem("drive_ready"), sem("scan_ready")
        last_ready, ch_ready, summed, gated = sem("last_ready"), sem("ch_ready"), sem("summed"), sem("gated")
        x1_ready, gap_ready, ratio_ready, comb_ready = (
            sem(n) for n in ("x1_ready", "gap_ready", "ratio_ready", "comb_ready"))
        tile_ready, g_ready, hg_ready, hg_used, unit_added = (
            sem(n) for n in ("tile_ready", "g_ready", "hg_ready", "hg_used", "unit_added"))

        def wait(eng, s, value):
            if not (isinstance(value, int) and value <= 0):
                eng.wait_ge(s, value)

        def tile_count(b, tile):
            return before(b, lambda i: len(tiles_of(i))) + tiles_of(b).index(tile) + 1

        def tile_wait(eng, b, tile):
            wait(eng, scratch_ready, tile_count(b, tile))

        def left_wait(eng, b, tile):
            wait(eng, scratch_free, tile_count(b, tile))

        def last_count(b, k):
            s, n = divmod(k, N)
            d, c = divmod(s, NC)
            return b * 2 * (NC - 1) * N + (d * (NC - 1) + c) * N + n + 1

        mamba_loads = [
            (ident[:], a["ident"]), (flip[:], a["flip"]), (pick[:], a["pick"]), (prio[:], a["prio"]),
            (gamma[:], a["gamma"].rearrange("(p o) -> p o", o=1)), (beta[:], a["beta"].rearrange("(p o) -> p o", o=1)),
        ]
        for i, d in enumerate(DIRS):
            mamba_loads += [
                (in_w[:, i, :], a[d + "in_w"]),
                (conv_w[:, i], a[d + "conv_w"].rearrange("(h p) t -> p h t", p=P)),
                (conv_b[:, i], a[d + "conv_b"]),
                (dt_w[3 * BC:XR, i, :], a[d + "dt_w"]),
                (dt_b[:, i], a[d + "dt_b"]),
                (a_log[:, i], a[d + "A_log"].rearrange("(h p) n -> p h n", p=P)),
                (d_skip[:, i], a[d + "D"]),
                (out_w[:, i], a[d + "out_w"].rearrange("(h p) d -> p h d", p=P)),
                (xproj[:, i, :, 3 * BC:XR], a[d + "xproj_w"][:, 0:R].rearrange("(h p) r -> p h r", p=P)),
            ]
            for c in range(3):
                mamba_loads.append((xproj[:, i, :, c * BC:(c + 1) * BC],
                                    a[d + "xproj_w"][:, R:R + BC].rearrange("(h p) r -> p h r", p=P)))
        ffn_loads = [
            (wg[:], a["Wg"]), (bg[:], a["bg"].rearrange("(o e) -> o e", o=1).to_broadcast([P, E])),
            (w0[:], a["W0"].rearrange("e d h -> d e h")), (w1[:], a["W1"].rearrange("e d h -> d e h")),
            (w2[:], a["W2"].rearrange("e (j p) d -> p e j d", p=P)),
            (b0[:], a["b0"]), (b1[:], a["b1"]),
            (b2[:], a["b2"]),
        ]

        block = ctx.enter_context(nc.Block())

        @block.sync
        def _(sp):
            sp.sem_inc(stored, 16)
            sp.dma_start(xn[:], x_rows[0]).then_inc(x_loaded, 16)
            for dst, src in mamba_loads:
                sp.dma_start(dst, src).then_inc(mamba_loaded, 16)
            sp.dma_start(res[:], x_rows[0]).then_inc(res_loaded, 16)
            for dst, src in ffn_loads:
                sp.dma_start(dst, src).then_inc(ffn_loaded, 16)
            for b in range(-1, B + 1):
                if 0 < b < B:
                    sp.wait_ge(x1_ready, b)
                    sp.dma_start(res[:], x_rows[b]).then_inc(res_loaded, 16)
                if b + 2 < B:
                    tile_wait(sp, b, ("xnT", 1, 0, 2 * NC - 1))
                    sp.dma_start(xn[:], x_rows[b + 2]).then_inc(x_loaded, 16)
                if b > 0:
                    sp.wait_ge(rows_ready, b)
                    sp.dma_start(out_rows[b - 1], x1[:]).then_inc(stored, 16)
            sp.wait_ge(stored, 16 * (B + 1))

        @block.tensor
        def _(pe):
            claimed = []

            def claim(b, c_step=None):
                if not claimed or claimed[-1][0] == "C":
                    ahead = c_step if c_step is not None else 0 if b < 0 else B * STEPS
                    wait(pe, c_copied, claimed[-1][1] if claimed else ahead)
                if not claimed or claimed[-1][0] != "C":
                    mine = len([t for t in claimed if t[0] != "C"])
                    wait(pe, scratch_free, before(b, lambda i: len(tiles_of(i))) + mine)
                claimed.append(("tile",) if c_step is None else ("C", c_step + 1))

            def replicate(b, q, k):
                s, n = divmod(k, N)
                if n == 0:
                    wait(pe, parts_ready, q * NSEG + s + 1)
                wait(pe, drive_ready, q * STEPS + k - 1)
                pe.matmul(b_rep[:, k % 2, :], pick[:, n, :], parts[:, s % 2, :],
                          start=True, stop=True).then_inc(b_ready, 1)
                claim(b, q * STEPS + k)
                pe.matmul(scratch[:], pick[:, N + n, :], parts[:, s % 2, :],
                          start=True, stop=True).then_inc(c_ready, 1)

            def sum_states(b, q, k):
                s, n = divmod(k, N)
                if n == 0:
                    wait(pe, gated, q * NSEG + s)
                    wait(pe, du_ready, q * NSEG + s + 1)
                    for i in range(CB):
                        for h in range(NH):
                            pe.matmul(y_acc[:, i, h * P:(h + 1) * P], du[:, h, i * P:(i + 1) * P], ident[:],
                                      start=(i % 2 == 0 and h == 0), stop=False, is_transpose=True,
                                      skip_group_check=True)
                wait(pe, ch_ready, q * STEPS + k + 1)
                for i in range(CB):
                    for h in range(NH):
                        mm = pe.matmul(y_acc[:, i, h * P:(h + 1) * P], state[:, k % 4, h, i * P:(i + 1) * P],
                                       ident[:], start=False, stop=(n == N - 1), is_transpose=True,
                                       skip_group_check=True)
                mm.then_inc(summed, 1)

            def scratch_tile(b, q, name, s, i):
                d, c = divmod(s, NC)
                if name == "xnT":
                    if i == 0:
                        wait(pe, xn_ready, q + 1)
                    claim(b)
                    d, g = divmod(i, NC)
                    for j in range(CB):
                        r = g * CB + j
                        mm = pe.transpose(scratch[:, j * P:(j + 1) * P], xn[:, (BLK - 1 - r) if d else r, :],
                                          (flip if d else ident)[:])
                elif name == "u":
                    claim(b)
                    mm = pe.matmul(scratch[:], in_w[:, d, i * P:(i + 1) * P], xnT[:, d, c * CH:(c + 1) * CH],
                                   start=True, stop=True)
                elif name == "z":
                    claim(b)
                    for j in range(2):
                        t0 = c * CH + (2 * i + j) * P
                        mm = pe.matmul(scratch[:, j * DI:(j + 1) * DI], xnT[:, d, t0:t0 + P],
                                       in_w[:, d, DI:2 * DI], start=True, stop=True)
                elif name == "xdbl":
                    wait(pe, uc_ready, q * NSEG + s + 1)
                    claim(b)
                    for h in range(NH):
                        mm = pe.matmul(scratch[0:XR, :], xproj[:, d, h, :], uc[:, h, :], start=(h == 0),
                                       stop=(h == NH - 1))
                elif name == "dt":
                    if i == 0:
                        wait(pe, hi_ready, q * NSEG + s + 1)
                    claim(b)
                    mm = pe.matmul(scratch[:], dt_w[3 * BC:XR, d, i * P:(i + 1) * P], dt_low[3 * BC:XR, :],
                                   start=True, stop=True)
                elif name == "turn":
                    if i == 0:
                        wait(pe, gated, q * NSEG + s + 1)
                    claim(b)
                    for j in range(CB):
                        at = CB - 1 - j if d else j
                        mm = pe.transpose(scratch[:, at * P:(at + 1) * P],
                                          gate[:, s % 2, j, i * P:(i + 1) * P], (flip if d else ident)[:])
                elif name == "out":
                    claim(b)
                    for j in range(CB):
                        for h in range(NH):
                            mm = pe.matmul(scratch[:, j * D:(j + 1) * D], y_turn[:, h, j * P:(j + 1) * P],
                                           out_w[:, d, h, :], start=(h == 0), stop=(h == NH - 1))
                elif name == "x1T":
                    if i == 0:
                        wait(pe, x1_ready, q + 1)
                    claim(b)
                    for j in range(CB):
                        mm = pe.transpose(scratch[:, j * P:(j + 1) * P], x1[:, i * CB + j, :], ident[:])
                elif name == "logits":
                    claim(b)
                    for j in range(BLK):
                        mm = pe.matmul(scratch[:, j * E:(j + 1) * E], x1T[:, j * P:(j + 1) * P], wg[:],
                                       start=True, stop=True)
                elif name == "combT":
                    if i == 0:
                        wait(pe, comb_ready, q + 1)
                    claim(b)
                    for j in range(CB):
                        mm = pe.matmul(scratch[0:E, j * P:(j + 1) * P], comb[:, i * CB + j, :], ident[:],
                                       start=True, stop=True)
                elif name == "b2":
                    claim(b)
                    for j in range(CB):
                        r = i * CB + j
                        mm = pe.matmul(scratch[:, j * D:(j + 1) * D], combT[:, r * P:(r + 1) * P], b2[:],
                                       start=True, stop=True)
                mm.then_inc(scratch_ready, 1)

            def ffn_tile(q, kind, sub):
                at = FFN_AT[(kind, sub)]
                if at >= 2:
                    old = FFN[at - 2]
                    wait(pe, g_ready if old[0] == "g" else hg_ready, q * SUBS + old[1] + 1)
                u, j = divmod(sub, HB)
                c, e = divmod(u, E)
                pe.matmul(ffn_in[:, at % 2, :], (w1 if kind == "g" else w0)[:, e, j * P:(j + 1) * P],
                          x1T[:, c * CH:(c + 1) * CH], start=True, stop=True).then_inc(tile_ready, 1)

            def down(q, sub):
                u, j = divmod(sub, HB)
                wait(pe, hg_ready, q * SUBS + sub + 1)
                if j == 0 and u:
                    wait(pe, unit_added, q * UNITS + u)
                for i in range(CB):
                    mm = pe.matmul(ffn_out[:, i, :], hg[:, sub % 2, i * P:(i + 1) * P], w2[:, u % E, j, :],
                                   start=(j == 0 and i == 0), stop=(j == HB - 1), skip_group_check=True)
                mm.then_inc(hg_used, 1)

            def iteration(b):
                claimed.clear()
                for name, off, *arg in events_of(b):
                    if name == "replicate":
                        replicate(b, b + off, *arg)
                    elif name == "sum":
                        sum_states(b, b + off, *arg)
                    elif name in SCRATCH_TILES:
                        scratch_tile(b, b + off, name, *arg)
                    elif name == "gates":
                        for j in range(HB):
                            ffn_tile(b + off, "g", arg[0] * HB + j)
                    elif name == "hidden":
                        ffn_tile(b + off, "h", *arg)
                    elif name == "down":
                        down(b + off, *arg)

            pe.wait_ge(mamba_loaded, 16 * len(mamba_loads))
            pe.wait_ge(ffn_loaded, 16 * len(ffn_loads))
            iterations(pe, iteration)

        @block.scalar
        def _(act):
            def exp_ln_tables():
                act.preload_act_table_set(EXP_LN_TABLES)

            def copy_c(q, k):
                wait(act, ch_ready, q * STEPS + k - 3)
                wait(act, c_ready, q * STEPS + k + 1)
                act.activation(c_rep[:, k % 4, :], scratch[:], ACT.Copy).then_inc(c_copied, 1)

            def decays(q, k):
                s, n = divmod(k, N)
                if n == 0:
                    wait(act, dt_ready, q * NSEG + s + 1)
                wait(act, scan_ready, q * STEPS + k - 3)
                for h in range(NH):
                    e = act.activation(decay[:, k % 4, h, :], dt[:, s % 2, h, :], ACT.Exp,
                                       scale=a_neg[:, s // NC, h, n:n + 1])
                e.then_inc(decay_ready, 1)

            def root(b, event):
                nth = before(b, lambda i: len(norms_of(i))) + norms_of(b).index(event)
                wait(act, var_ready, nth + 1)
                act.activation(rstd[:], var[:], ACT.Ln).then_inc(log_ready, 1)
                wait(act, log_ready, nth + 1)
                act.activation(rstd[:], rstd[:], ACT.Exp, scale=-0.5).then_inc(root_ready, 1)

            def gates(q, u):
                if u >= 2:
                    wait(act, hg_ready, q * SUBS + (u - 1) * HB)
                for j in range(HB):
                    at = FFN_AT[("g", u * HB + j)]
                    wait(act, tile_ready, q * 2 * SUBS + at + 1)
                    act.activation(g_act[:, u % 2, j, :], ffn_in[:, at % 2, :], ACT.Silu,
                                   bias=b1[:, u % E, j:j + 1]).then_inc(g_ready, 1)
                exp_ln_tables()

            def scratch_tile(b, q, event):
                name, off, s, i = event
                d, c = divmod(s, NC)
                if name not in ("out", "logits", "b2"):
                    tile_wait(act, b, event)
                if name == "xnT":
                    act.activation(xnT[:, i // NC, (i % NC) * CH:(i % NC + 1) * CH], scratch[:], ACT.Identity,
                                   bias=beta[:], scale=gamma[:]).then_inc(scratch_free, 1)
                elif name == "u":
                    wait(act, conv_ready, q * NSEG + s)
                    t0 = TAPS - 1 + c * CH
                    act.activation(u_pad[:, i, t0:t0 + CH], scratch[:], ACT.Copy).then_inc(scratch_free, 1)
                elif name == "z":
                    act.activation(gate[:, s % 2, 2 * i:2 * i + 2, :],
                                   scratch[:].rearrange("p (i e) -> p i e", i=2), ACT.Silu).then_inc(scratch_free, 1)
                    if i == 1:
                        wait(act, conv_ready, q * NSEG + s + 1)
                        act.activation(uc[:], uc[:], ACT.Silu).then_inc(uc_ready, 1)
                        exp_ln_tables()
                elif name == "xdbl":
                    act.activation(parts[:, s % 2, :], scratch[0:3 * BC, :], ACT.Copy)
                    act.activation(dt_low[3 * BC:XR, :], scratch[3 * BC:XR, :], ACT.Copy).then_inc(hi_ready, 1)
                elif name == "dt":
                    wait(act, drive_ready, q * STEPS + N * (s - 1))
                    act.activation(dtu[:, s % 2, i, :], scratch[:], ACT.Identity, bias=dt_b[:, d, i:i + 1])
                    act.activation(dt[:, s % 2, i, :], scratch[:], ACT.Abs,
                                   bias=dt_b[:, d, i:i + 1]).then_inc(scratch_free, 1)
                    if i == NH - 1:
                        left_wait(act, b, event)
                        act.activation(dt[:, s % 2], dt[:, s % 2], ACT.Exp, scale=-1.0).then_inc(exp_ready, 1)
                        wait(act, exp_ready, q * NSEG + s + 1)
                        act.activation(dt[:, s % 2], dt[:, s % 2], ACT.Ln, bias=1.0).then_inc(soft_ready, 1)
                elif name == "turn":
                    act.activation(y_turn[:, i, :], scratch[:], ACT.Copy).then_inc(scratch_free, 1)
                elif name == "x1T":
                    act.activation(x1T[:, i * CH:(i + 1) * CH], scratch[:], ACT.Copy).then_inc(scratch_free, 1)
                elif name == "combT":
                    if not isinstance(b, int) or b < B:
                        wait(act, dtu_ready, b * NSEG + 2)
                    act.activation(combT[:, i * CH:(i + 1) * CH], scratch[0:E, :], ACT.Copy).then_inc(scratch_free, 1)

            def iteration(b):
                for event in events_of(b):
                    name, off, *arg = event
                    if name == "replicate":
                        copy_c(b + off, *arg)
                    elif name == "decay":
                        decays(b + off, *arg)
                    elif name == "spread":
                        root(b, event)
                    elif name == "split":
                        s = arg[0]
                        left_wait(act, b, ("xdbl", off, s, 0))
                        act.activation(parts[BC:2 * BC, s % 2, :], rest[BC:2 * BC, :], ACT.Copy)
                        act.activation(mid[2 * BC:, :], rest[2 * BC:3 * BC, :], ACT.Copy).then_inc(mid_ready, 1)
                    elif name == "comb":
                        wait(act, gap_ready, b + off + 1)
                        act.activation(ratio[:], gap[:], ACT.Exp).then_inc(ratio_ready, 1)
                    elif name == "gates":
                        gates(b + off, *arg)
                    elif name in SCRATCH_TILES:
                        scratch_tile(b, b + off, event)

            act.wait_ge(mamba_loaded, 16 * len(mamba_loads))
            exp_ln_tables()
            act.activation(a_exp[:], a_log[:], ACT.Exp).then_inc(a_ready, 1)
            act.wait_ge(a_ready, 1)
            act.activation(a_neg[:], a_exp[:], ACT.Copy, scale=-1.0).then_inc(a_ready, 1)
            act.wait_ge(a_ready, 2)
            act.wait_ge(ffn_loaded, 16 * len(ffn_loads))
            iterations(act, iteration)

        @block.gpsimd
        def _(pool):
            pool.memset(one[:], 1.0).then_inc(one_ready, 1)
            pool.wait_ge(one_ready, 1)
            with pool.Fori(0, B) as b:
                for k in range(STEPS):
                    s, n = divmod(k, N)
                    pool.wait_ge(scan_ready, b * STEPS + k + 1)
                    pool.wait_ge(c_copied, b * STEPS + k + 1)
                    if s % NC < NC - 1:
                        pool.tensor_tensor(last[:, n, :], state[:, k % 4, :, CH - 1], one[:],
                                           ALU.mult).then_inc(last_ready, 1)
                        pool.wait_ge(last_ready, last_count(b, k))
                    pool.tensor_tensor(state[:, k % 4], state[:, k % 4],
                                       c_rep[:, k % 4:k % 4 + 1, :].to_broadcast([P, NH, CH]),
                                       ALU.mult).then_inc(ch_ready, 1)

        @block.vector
        def _(dve):
            linked = [0]

            def links(b):
                return sum(LINKS.get(e[0], 0) for e in events_of(b))

            def link(b, ins):
                linked[0] += 1
                ins.then_inc(chain, 1)
                dve.wait_ge(chain, before(b, links) + linked[0])

            def spread_over(v):
                return v[:].rearrange("p (i o) -> p i o", o=1).to_broadcast([P, BLK, E])

            def stats_of(b, q, which):
                if which == 0:
                    wait(dve, x_loaded, 16 * (q + 1))
                elif which == 1:
                    left_wait(dve, b, ("out", -1, NSEG - 1, 0))
                else:
                    wait(dve, unit_added, (q + 1) * UNITS)
                for i in range(BLK):
                    ins = dve.bn_stats(stats[:, i, :], (xn, res, x1)[which][:, i, :])
                ins.then_inc(stats_ready, 1)

            def spread(b, event):
                nth = before(b, lambda i: len(norms_of(i))) + norms_of(b).index(event)
                wait(dve, stats_ready, nth + 1)
                dve.tensor_tensor(mean[:], stats[:, :, 1], stats[:, :, 4], ALU.add)
                dve.tensor_tensor(apart[:], stats[:, :, 1], stats[:, :, 4], ALU.subtract)
                link(b, dve.tensor_tensor(var[:], stats[:, :, 2], stats[:, :, 5], ALU.add))
                dve.tensor_scalar(mean[:], mean[:], 0.5, None, ALU.mult)
                dve.tensor_scalar(var[:], var[:], 1.0 / D, EPS, ALU.mult, ALU.add)
                link(b, dve.scalar_tensor_tensor(apart[:], apart[:], 0.25, apart[:], ALU.mult, ALU.mult))
                dve.tensor_tensor(var[:], var[:], apart[:], ALU.add).then_inc(var_ready, 1)

            def normal(b, q, which, nth):
                wait(dve, root_ready, nth + 1)
                link(b, dve.tensor_tensor(newton[:], var[:], rstd[:], ALU.mult))
                link(b, dve.tensor_tensor(newton[:], newton[:], rstd[:], ALU.mult))
                link(b, dve.tensor_scalar(newton[:], newton[:], -0.5, 1.5, ALU.mult, ALU.add))
                link(b, dve.tensor_tensor(rstd[:], rstd[:], newton[:], ALU.mult))
                src, dst, done = ((xn, xn, xn_ready), (res, x1, x1_ready), (x1, x1, rows_ready))[which]
                if which == 1:
                    wait(dve, stored, 16 * (q + 1))
                for i in range(BLK):
                    ins = dve.tensor_scalar(dst[:, i, :], src[:, i, :], mean[:, i:i + 1], rstd[:, i:i + 1],
                                            ALU.subtract, ALU.mult)
                ins.then_inc(done, 1)

            def drive_step(q, k):
                s, n = divmod(k, N)
                if n == 0:
                    wait(dve, dtu_ready, q * NSEG + s + 1)
                wait(dve, b_ready, q * STEPS + k + 1)
                wait(dve, scan_ready, q * STEPS + k - 1)
                dve.tensor_tensor(drive[:, k % 2], dtu[:, s % 2],
                                  b_rep[:, k % 2:k % 2 + 1, :].to_broadcast([P, NH, CH]),
                                  ALU.mult).then_inc(drive_ready, 1)

            def scan_step(q, k):
                s, n = divmod(k, N)
                wait(dve, drive_ready, q * STEPS + k + 1)
                wait(dve, decay_ready, q * STEPS + k + 1)
                wait(dve, summed, q * STEPS + k - 3)
                if s % NC:
                    wait(dve, last_ready, last_count(q, k - N))
                for h in range(NH):
                    ins = dve.tensor_tensor_scan(state[:, k % 4, h, :], decay[:, k % 4, h, :], drive[:, k % 2, h, :],
                                                 last[:, n, h:h + 1] if s % NC else 0.0, ALU.mult, ALU.add)
                ins.then_inc(scan_ready, 1)

            def convolve(b, q, s):
                d, c = divmod(s, NC)
                left_wait(dve, b, ("u", 1 if s == 0 else 0, s, 1))
                for t in reversed(range(TAPS)):
                    for h in range(NH):
                        taps = u_pad[:, h, c * CH + t:c * CH + t + CH]
                        w = conv_w[:, d, h, t:t + 1]
                        if t == TAPS - 1:
                            ins = dve.tensor_scalar(uc[:, h, :], taps, w, conv_b[:, d, h:h + 1], ALU.mult, ALU.add)
                        else:
                            ins = dve.scalar_tensor_tensor(uc[:, h, :], taps, w, uc[:, h, :], ALU.mult, ALU.add)
                    if t:
                        link(b, ins)
                ins.then_inc(conv_ready, 1)

            def times_u(q, s):
                wait(dve, soft_ready, q * NSEG + s + 1)
                dve.scalar_tensor_tensor(dt[:, s % 2], dtu[:, s % 2], 0.0, dt[:, s % 2], ALU.max,
                                         ALU.add).then_inc(dt_ready, 1)
                wait(dve, uc_ready, q * NSEG + s + 1)
                wait(dve, summed, q * STEPS + N * (s - 1) + 1)
                for h in range(NH):
                    ins = dve.tensor_scalar(du[:, h, :], uc[:, h, :], d_skip[:, s // NC, h:h + 1], None, ALU.mult)
                ins.then_inc(du_ready, 1)
                wait(dve, dt_ready, q * NSEG + s + 1)
                dve.tensor_tensor(dtu[:, s % 2], dt[:, s % 2], uc[:], ALU.mult).then_inc(dtu_ready, 1)

            def hidden(q, sub):
                u, j = divmod(sub, HB)
                at = FFN_AT[("h", sub)]
                wait(dve, tile_ready, q * 2 * SUBS + at + 1)
                wait(dve, g_ready, q * SUBS + sub + 1)
                if sub >= 2:
                    wait(dve, hg_used, q * SUBS + sub - 1)
                dve.scalar_tensor_tensor(hg[:, sub % 2, :], ffn_in[:, at % 2, :], b0[:, u % E, j:j + 1],
                                         g_act[:, u % 2, j, :], ALU.add, ALU.mult).then_inc(hg_ready, 1)

            def add_unit(b, q, u):
                c, e = divmod(u, E)
                wait(dve, hg_used, q * SUBS + HB * (u + 1))
                if u:
                    wait(dve, unit_added, q * UNITS + u)
                else:
                    left_wait(dve, b, ("b2", -1, 0, 1))
                for i in range(CB):
                    r = c * CB + i
                    ins = dve.scalar_tensor_tensor(x1[:, r, :], ffn_out[:, i, :], comb[:, r, e:e + 1], x1[:, r, :],
                                                   ALU.mult, ALU.add)
                ins.then_inc(unit_added, 1)

            def first_best(b, of, best, mask):
                link(b, dve.tensor_reduce(best[:], of[:], AX_X, ALU.max))
                link(b, dve.tensor_tensor(mask[:], of[:], spread_over(best), ALU.is_equal))
                link(b, dve.tensor_tensor(mask[:], mask[:], prio[:].rearrange("p (o e) -> p o e", o=1)
                                          .to_broadcast([P, BLK, E]), ALU.mult))
                link(b, dve.tensor_reduce(vmax[:], mask[:], AX_X, ALU.max))
                link(b, dve.tensor_tensor(mask[:], mask[:], spread_over(vmax), ALU.is_equal))

            def best_two(b):
                event = ("logits", -1, 0, 0)
                tile_wait(dve, b, event)
                dve.tensor_tensor(logits[:], scratch[:, 0:BLK * E].rearrange("p (i e) -> p i e", i=BLK),
                                  bg[:].rearrange("p (o e) -> p o e", o=1).to_broadcast([P, BLK, E]),
                                  ALU.add).then_inc(scratch_free, 1)
                left_wait(dve, b, event)
                first_best(b, logits, m1, first)
                link(b, dve.scalar_tensor_tensor(work[:], first[:], NEG, logits[:], ALU.mult, ALU.add))
                first_best(b, work, m2, second)
                dve.tensor_tensor(gap[:], m2[:], m1[:], ALU.subtract).then_inc(gap_ready, 1)

            def shares(b, q):
                dve.wait_ge(ratio_ready, q + 1)
                link(b, dve.tensor_scalar(wsum[:], ratio[:], 1.0, None, ALU.add))
                link(b, dve.reciprocal(weight1[:], wsum[:]))
                link(b, dve.tensor_tensor(weight2[:], weight1[:], ratio[:], ALU.mult))
                link(b, dve.tensor_tensor(first[:], first[:], spread_over(weight1), ALU.mult))
                link(b, dve.tensor_tensor(second[:], second[:], spread_over(weight2), ALU.mult))
                dve.tensor_tensor(comb[:], first[:], second[:], ALU.add).then_inc(comb_ready, 1)

            def scratch_rows(i):
                return scratch[:].rearrange("p (i e) -> p i e", i=i)

            def iteration(b):
                linked[0] = 0
                for event in events_of(b):
                    name, off, *arg = event
                    q = b + off
                    if name == "drive":
                        drive_step(q, *arg)
                    elif name == "scan":
                        scan_step(q, *arg)
                    elif name == "stats":
                        stats_of(b, q, arg[1])
                    elif name == "spread":
                        spread(b, event)
                    elif name == "normal":
                        nth = before(b, lambda i: len(norms_of(i))) + norms_of(b).index(("spread", off, *arg))
                        normal(b, q, arg[1], nth)
                    elif name == "conv":
                        convolve(b, q, arg[0])
                    elif name == "xdbl":
                        s = arg[0]
                        wait(dve, hi_ready, q * NSEG + s + 1)
                        dve.tensor_tensor(rest[0:3 * BC, :], scratch[0:3 * BC, :], parts[:, s % 2, :],
                                          ALU.subtract).then_inc(scratch_free, 1)
                    elif name == "split":
                        s = arg[0]
                        wait(dve, mid_ready, q * NSEG + s + 1)
                        dve.tensor_tensor(parts[2 * BC:, s % 2, :], rest[2 * BC:3 * BC, :], mid[2 * BC:, :],
                                          ALU.subtract).then_inc(parts_ready, 1)
                    elif name == "dtu":
                        times_u(q, arg[0])
                    elif name == "gate":
                        s = arg[0]
                        wait(dve, summed, q * STEPS + N * (s + 1))
                        for g in range(2):
                            ins = dve.tensor_tensor(gate[:, s % 2, 2 * g:2 * g + 2, :], y_acc[:, 2 * g:2 * g + 2, :],
                                                    gate[:, s % 2, 2 * g:2 * g + 2, :], ALU.mult)
                        ins.then_inc(gated, 1)
                    elif name == "out":
                        d, c = divmod(arg[0], NC)
                        at = CB * (NC - 1 - c if d else c)
                        wait(dve, res_loaded, 16 * (q + 1))
                        if d:
                            wait(dve, scratch_free, tile_count(b, event) - 1)
                        tile_wait(dve, b, event)
                        dve.scalar_tensor_tensor(res[:, at:at + CB, :], res[:, at:at + CB, :], 1.0 if d else 2.0,
                                                 scratch_rows(CB), ALU.mult, ALU.add).then_inc(scratch_free, 1)
                    elif name == "logits":
                        best_two(b)
                    elif name == "comb":
                        shares(b, q)
                    elif name == "b2":
                        tile_wait(dve, b, event)
                        rows = x1[:, arg[1] * CB:(arg[1] + 1) * CB, :]
                        dve.tensor_tensor(rows, scratch_rows(CB), rows, ALU.add).then_inc(scratch_free, 1)
                    elif name == "hidden":
                        hidden(q, *arg)
                    elif name == "add":
                        add_unit(b, q, *arg)
                assert not isinstance(b, int) or linked[0] == links(b), (linked, links(b))

            dve.memset(u_pad[:, :, 0:TAPS - 1], 0.0).then_inc(pad_ready, 1)
            dve.wait_ge(pad_ready, 1)
            dve.wait_ge(mamba_loaded, 16 * len(mamba_loads))
            dve.wait_ge(ffn_loaded, 16 * len(ffn_loads))
            iterations(dve, iteration)


def kernel(**inputs):
    import numpy as _np
    import concourse.bacc as _bacc
    from concourse import mybir as _mybir
    from concourse.bass_utils import run_bass_kernel_spmd as _run

    def flat(v):
        return _np.ascontiguousarray(v)

    laid = {"x": flat(inputs["L0_attn_x"]), "gamma": flat(inputs["L0_attn_gamma"]), "beta": flat(inputs["L0_attn_beta"])}
    for d in ("f_", "b_"):
        pre = "L0_attn_" + d
        for name in ("in_w", "xproj_w", "dt_w", "out_w"):
            laid[d + name] = flat(_np.asarray(inputs[pre + name]).T)
        laid[d + "conv_w"] = flat(_np.asarray(inputs[pre + "conv_w"])[:, 0, :])
        laid[d + "A_log"] = flat(inputs[pre + "A_log"])
        for name in ("conv_b", "dt_b", "D"):
            laid[d + name] = flat(_np.asarray(inputs[pre + name]).reshape(NH, P).T)
    for name in ("Wg", "bg", "W0", "W1", "W2", "b2"):
        laid[name] = flat(inputs["L0_ffn_" + name])
    for name in ("b0", "b1"):
        laid[name] = flat(_np.asarray(inputs["L0_ffn_" + name]).reshape(E, HB, P).transpose(2, 0, 1))
    laid["ident"] = _np.eye(P, dtype=_np.float32)
    laid["flip"] = flat(_np.eye(P, dtype=_np.float32)[::-1])
    rows = _np.arange(3 * BC)[:, None, None] % BC == _np.arange(BC)[None, :, None]
    import ml_dtypes as _ml
    laid["pick"] = flat(_np.broadcast_to(rows, (3 * BC, BC, P)).astype(_ml.bfloat16))
    laid["prio"] = flat(_np.broadcast_to(_np.arange(E, 0, -1, dtype=_np.float32), (P, E)))

    nc = _bacc.Bacc("TRN2", target_bir_lowering=False, num_devices=1)
    arrays, args = {}, {}
    for name, v in laid.items():
        arrays[f"in_{name}"] = v
        args[name] = nc.dram_tensor(f"in_{name}", v.shape, _mybir.dt.from_np(v.dtype), kind="ExternalInput").ap()
    out = nc.dram_tensor("out_0", (B, L, D), F32, kind="ExternalOutput").ap()
    build(nc, args, out)
    r = _run(nc, [arrays], core_ids=[0])
    return r.results[0]["out_0"]
```

```python
from contextlib import ExitStack

import concourse.bass as bass
import numpy as np
from concourse import mybir

F32 = mybir.dt.float32
BF16 = mybir.dt.bfloat16
ALU = mybir.AluOpType
ACT = mybir.ActivationFunctionType
AX_X = mybir.AxisListType.X
EXP_LN_TABLES = "natural_log_exp_and_others"

B, L, D = 8, 1024, 128
P = 128
DI = 2 * D
NH = DI // P
N = 16
TAPS = 4
R = 8
CH = 512
NC = L // CH
BLK = L // P
CB = CH // P
NSEG = 2 * NC
STEPS = NSEG * N
E = 8
HID = 512
HB = HID // P
UNITS = NC * E
SUBS = UNITS * HB
EPS = 1e-5
NEG = -3.0e38
BC = 2 * N
XR = 3 * BC + R
DIRS = ("f_", "b_")

PREPARE = {0: ("u", 0), 1: ("u", 1), 2: ("conv", 0), 8: ("xdbl", 0), 9: ("rest", 0),
           10: ("dt", 0), 11: ("dt", 1), 12: ("low", 0), 13: ("dtu", 0)}
Z_SLOTS = {6: 1, 23: 2, 38: 3, 53: 0}
FINISH = {1: ("gate", 0), 2: ("turn", 0), 3: ("turn", 1), 4: ("out", 0), 5: ("residual", 0)}
NEXT_NORM = {17: ("stats", 0), 18: ("spread", 0), 20: ("normal", 0), 29: ("xnT", 0), 30: ("xnT", 1),
             45: ("xnT", 2), 46: ("xnT", 3)}
ROUTE = {6: ("stats", 1), 7: ("spread", 1), 8: ("normal", 1), 9: ("x1T", 0), 10: ("logits", 0), 11: ("best", 0),
         12: ("comb", 0), 13: ("combT", 0), 14: ("b2", 0)}
SECOND = ("x1T", "combT", "b2")
OUT_NORM = {61: ("stats", 2), 62: ("spread", 2), 63: ("normal", 2)}
FFN_FROM = 11


def slot_events(k):
    def at(step):
        return step // STEPS, step % STEPS

    seg, local = divmod(k, N)
    u, r = divmod(k - FFN_FROM, 3)
    events = [("c_row", *at(k + 2)), ("decay", *at(k + 2))]
    hidden = [("hidden", -1, u * HB + j) for j in ((), (0, 1), (2, 3))[r] if 0 <= u < UNITS]
    events += hidden
    events += [("drive", *at(k + 1)), ("scan", 0, k), ("sum", *at(k - 2))]
    tiles = []
    if local in FINISH:
        name, i = FINISH[local]
        tiles.append((name, (seg - 1) // NSEG, (seg - 1) % NSEG, i))
    if local in PREPARE:
        name, i = PREPARE[local]
        tiles.append((name, (seg + 1) // NSEG, (seg + 1) % NSEG, i))
        if name == "dt" and i == 0:
            tiles.append(("mid", (seg + 1) // NSEG, (seg + 1) % NSEG, 0))
    for table, off in ((NEXT_NORM, 1), (ROUTE, -1), (OUT_NORM, -1)):
        if k in table:
            tiles.append((table[k][0], off, 0, table[k][1]))
    events += tiles
    for du, j in ((), ((-1, 2), (-1, 3)), ((0, 0), (0, 1)))[r]:
        if 0 <= u + du < UNITS:
            events.append(("down", -1, (u + du) * HB + j))
    events += [("product",) + e[1:] for e in hidden]
    if r == 1 and 0 <= u - 1 < UNITS:
        events.append(("add", -1, u - 1))
    later = [(e[0], e[1], e[2], 1) for e in tiles if e[0] in SECOND]
    if k in Z_SLOTS:
        s = Z_SLOTS[k]
        events.append(("z", 0 if s else 1, s, 0))
    if r == 0 and 0 <= u < UNITS:
        events.append(("gates", -1, u))
    if k in Z_SLOTS:
        s = Z_SLOTS[k]
        later.append(("z", 0 if s else 1, s, 1))
    events.append(("b_row", *at(k + 2)))
    return events + later


ITERATION = [e for k in range(STEPS) for e in slot_events(k)]
SCRATCH_TILES = ("u", "z", "xdbl", "dt", "turn", "out", "xnT", "x1T", "logits", "combT", "b2")
LINKS = {"conv": TAPS - 1, "spread": 2, "normal": 4, "stats": 0, "best": 12, "comb": 5}


def events_of(b):
    return [e for e in ITERATION if not isinstance(b, int) or 0 <= b + e[1] < B]


def before(b, count):
    if isinstance(b, int):
        return sum(count(i) for i in range(-1, b))
    return before(1, count) + (b - 1) * count(1)


def tiles_of(b):
    return [e for e in events_of(b) if e[0] in SCRATCH_TILES]


def norms_of(b):
    return [e for e in events_of(b) if e[0] == "spread"]


def iterations(eng, do):
    do(-1)
    do(0)
    with eng.Fori(1, B - 1) as b:
        do(b)
    do(B - 1)
    do(B)


FFN = [("g", HB * e[2] + j) if e[0] == "gates" else ("h", e[2]) for e in ITERATION
       if e[0] in ("gates", "hidden") for j in range(HB if e[0] == "gates" else 1)]
FFN_AT = {t: i for i, t in enumerate(FFN)}
HG_SLOTS = 4
FFN_BANKS = 3
assert len(FFN) == 2 * SUBS


def build(nc, a, out):
    x_rows = a["x"].rearrange("b (c p) d -> b p c d", p=P)
    out_rows = out.rearrange("b (c p) d -> b p c d", p=P)

    with ExitStack() as ctx:
        def sb(name, shape, dt=F32):
            return ctx.enter_context(nc.sbuf_tensor(name, shape, dt))

        def psum(name, shape, dt=F32):
            return ctx.enter_context(nc.psum_tensor(name, shape, dt))

        def sem(name):
            return ctx.enter_context(nc.semaphore(name))

        ident = sb("ident", [P, P])
        flip = sb("flip", [P, P])
        pick = sb("pick", [3 * BC, BC], BF16)
        prio = sb("prio", [P, E])
        in_w = sb("in_w", [P, 2, 2 * DI])
        conv_w = sb("conv_w", [P, 2, NH, TAPS])
        conv_b = sb("conv_b", [P, 2, NH])
        xproj = sb("xproj", [P, 2, NH, XR])
        dt_w = sb("dt_w", [XR, 2, DI])
        dt_b = sb("dt_b", [P, 2, NH])
        a_log = sb("a_log", [P, 2, NH, N])
        a_exp = sb("a_exp", [P, 2, NH, N])
        a_neg = sb("a_neg", [P, 2, NH, N])
        d_skip = sb("d_skip", [P, 2, NH])
        out_w = sb("out_w", [P, 2, NH, D])
        gamma = sb("gamma", [P, 1])
        beta = sb("beta", [P, 1])
        wg = sb("wg", [P, E])
        bg = sb("bg", [P, E])
        w0 = sb("w0", [P, E, HID])
        w1 = sb("w1", [P, E, HID])
        w2 = sb("w2", [P, E, HB, D])
        b0 = sb("b0", [P, E, HB])
        b1 = sb("b1", [P, E, HB])
        b2 = sb("b2", [E, D])

        xn = sb("xn", [P, BLK, D])
        res = sb("res", [P, BLK, D])
        stats = sb("stats", [P, BLK, 6])
        mean = sb("mean", [P, BLK])
        apart = sb("apart", [P, BLK])
        rstd = sb("rstd", [P, BLK])
        var = sb("var", [P, BLK])
        newton = sb("newton", [P, BLK])
        xnT = sb("xnT", [P, 2, L])
        u_pad = sb("u_pad", [P, NH, TAPS - 1 + L])
        uc = sb("uc", [P, NH, CH])
        gate = sb("gate", [P, 2, CB, DI])
        parts = sb("parts", [3 * BC, 2, CH], BF16)
        rest = sb("rest", [P, CH])
        dt_low = rest
        mid = sb("mid", [3 * BC, CH], BF16)
        dt = sb("dt", [P, 2, NH, CH])
        dtu = sb("dtu", [P, 2, NH, CH])
        du = sb("du", [P, NH, CH])
        decay = sb("decay", [P, 4, NH, CH])
        c_rep = sb("c_rep", [P, 4, CH])
        drive = sb("drive", [P, 2, NH, CH])
        state = sb("state", [P, 4, NH, CH])
        last = sb("last", [P, N, NH])
        one = sb("one", [P, NH])
        y_turn = du

        x1 = sb("x1", [P, BLK, D])
        x1T = sb("x1T", [P, L])
        logits = sb("logits", [P, BLK, E])
        work = sb("work", [P, BLK, E])
        first = sb("first", [P, BLK, E])
        second = sb("second", [P, BLK, E])
        comb = sb("comb", [P, BLK, E])
        m1 = sb("m1", [P, BLK])
        m2 = sb("m2", [P, BLK])
        vmax = sb("vmax", [P, BLK])
        gap = sb("gap", [P, BLK])
        ratio = sb("ratio", [P, BLK])
        wsum = sb("wsum", [P, BLK])
        weight1 = sb("weight1", [P, BLK])
        weight2 = sb("weight2", [P, BLK])
        combT = uc[0:E].rearrange("e h t -> e (h t)")
        g_act = sb("g_act", [P, 2, HB, CH])
        hg = sb("hg", [P, HG_SLOTS, CH])

        b_rep = psum("b_rep", [P, CH])
        scratch = psum("scratch", [P, CH])
        y_acc = psum("y_acc", [P, CB, DI])
        ffn_in = psum("ffn_in", [P, FFN_BANKS, CH])
        ffn_out = psum("ffn_out", [P, CB, D])

        mamba_loaded, ffn_loaded = sem("mamba_loaded"), sem("ffn_loaded")
        x_loaded, res_loaded, rows_ready, stored = (sem(n) for n in ("x_loaded", "res_loaded", "rows_ready", "stored"))
        a_ready, one_ready, pad_ready = sem("a_ready"), sem("one_ready"), sem("pad_ready")
        stats_ready, var_ready, log_ready, root_ready = sem("stats_ready"), sem("var_ready"), sem("log_ready"), sem("root_ready")
        scratch_ready, scratch_free, chain = sem("scratch_ready"), sem("scratch_free"), sem("chain")
        xn_ready, conv_ready, uc_ready = sem("xn_ready"), sem("conv_ready"), sem("uc_ready")
        hi_ready, rest_ready, mid_ready, parts_ready = sem("hi_ready"), sem("rest_ready"), sem("mid_ready"), sem("parts_ready")
        exp_ready, soft_ready, dt_ready = sem("exp_ready"), sem("soft_ready"), sem("dt_ready")
        dtu_ready, du_ready = sem("dtu_ready"), sem("du_ready")
        b_ready, c_ready, c_copied = sem("b_ready"), sem("c_ready"), sem("c_copied")
        decay_ready, drive_ready, scan_ready = sem("decay_ready"), sem("drive_ready"), sem("scan_ready")
        summed_rows = sem("summed_rows")
        last_ready, ch_ready, summed, gated = sem("last_ready"), sem("ch_ready"), sem("summed"), sem("gated")
        x1_ready, gap_ready, ratio_ready, comb_ready = (
            sem(n) for n in ("x1_ready", "gap_ready", "ratio_ready", "comb_ready"))
        tile_ready, g_ready, hg_ready, hg_used, unit_added = (
            sem(n) for n in ("tile_ready", "g_ready", "hg_ready", "hg_used", "unit_added"))

        def wait(eng, s, value):
            if not (isinstance(value, int) and value <= 0):
                eng.wait_ge(s, value)

        def tile_count(b, tile):
            return before(b, lambda i: len(tiles_of(i))) + tiles_of(b).index(tile) + 1

        def tile_wait(eng, b, tile):
            wait(eng, scratch_ready, tile_count(b, tile))

        def left_wait(eng, b, tile):
            wait(eng, scratch_free, tile_count(b, tile))

        def last_count(b, k):
            s, n = divmod(k, N)
            d, c = divmod(s, NC)
            return b * 2 * (NC - 1) * N + (d * (NC - 1) + c) * N + n + 1

        mamba_loads = [
            (ident[:], a["ident"]), (flip[:], a["flip"]), (pick[:], a["pick"]), (prio[:], a["prio"]),
            (gamma[:], a["gamma"].rearrange("(p o) -> p o", o=1)), (beta[:], a["beta"].rearrange("(p o) -> p o", o=1)),
        ]
        for i, d in enumerate(DIRS):
            mamba_loads += [
                (in_w[:, i, :], a[d + "in_w"]),
                (conv_w[:, i], a[d + "conv_w"].rearrange("(h p) t -> p h t", p=P)),
                (conv_b[:, i], a[d + "conv_b"]),
                (dt_w[3 * BC:XR, i, :], a[d + "dt_w"]),
                (dt_b[:, i], a[d + "dt_b"]),
                (a_log[:, i], a[d + "A_log"].rearrange("(h p) n -> p h n", p=P)),
                (d_skip[:, i], a[d + "D"]),
                (out_w[:, i], a[d + "out_w"].rearrange("(h p) d -> p h d", p=P)),
                (xproj[:, i, :, 3 * BC:XR], a[d + "xproj_w"][:, 0:R].rearrange("(h p) r -> p h r", p=P)),
            ]
            for c in range(3):
                mamba_loads.append((xproj[:, i, :, c * BC:(c + 1) * BC],
                                    a[d + "xproj_w"][:, R:R + BC].rearrange("(h p) r -> p h r", p=P)))
        ffn_loads = [
            (wg[:], a["Wg"]), (bg[:], a["bg"].rearrange("(o e) -> o e", o=1).to_broadcast([P, E])),
            (w0[:], a["W0"].rearrange("e d h -> d e h")), (w1[:], a["W1"].rearrange("e d h -> d e h")),
            (w2[:], a["W2"].rearrange("e (j p) d -> p e j d", p=P)),
            (b0[:], a["b0"]), (b1[:], a["b1"]),
            (b2[:], a["b2"]),
        ]

        block = ctx.enter_context(nc.Block())

        @block.sync
        def _(sp):
            sp.sem_inc(stored, 16)
            sp.dma_start(xn[:], x_rows[0]).then_inc(x_loaded, 16)
            for dst, src in mamba_loads:
                sp.dma_start(dst, src).then_inc(mamba_loaded, 16)
            sp.dma_start(res[:], x_rows[0]).then_inc(res_loaded, 16)
            for dst, src in ffn_loads:
                sp.dma_start(dst, src).then_inc(ffn_loaded, 16)
            for b in range(-1, B + 1):
                if 0 < b < B:
                    sp.wait_ge(x1_ready, b)
                    sp.dma_start(res[:], x_rows[b]).then_inc(res_loaded, 16)
                if b + 2 < B:
                    tile_wait(sp, b, ("xnT", 1, 0, 2 * NC - 1))
                    sp.dma_start(xn[:], x_rows[b + 2]).then_inc(x_loaded, 16)
                if b > 0:
                    sp.wait_ge(rows_ready, b)
                    sp.dma_start(out_rows[b - 1], x1[:]).then_inc(stored, 16)
            sp.wait_ge(stored, 16 * (B + 1))

        @block.tensor
        def _(pe):
            claimed = []

            def claim(b, c_step=None):
                if not claimed or claimed[-1][0] == "C":
                    ahead = c_step if c_step is not None else 0 if b < 0 else B * STEPS
                    wait(pe, c_copied, claimed[-1][1] if claimed else ahead)
                if not claimed or claimed[-1][0] != "C":
                    mine = len([t for t in claimed if t[0] != "C"])
                    wait(pe, scratch_free, before(b, lambda i: len(tiles_of(i))) + mine)
                claimed.append(("tile",) if c_step is None else ("C", c_step + 1))

            def b_row(q, k):
                s, n = divmod(k, N)
                wait(pe, drive_ready, q * STEPS + k)
                pe.matmul(b_rep[:], pick[:, n:n + 1].to_broadcast([3 * BC, P]), parts[:, s % 2, :], start=True, stop=True).then_inc(b_ready, 1)

            def c_row(b, q, k):
                s, n = divmod(k, N)
                if n == 0:
                    pe.wait_ge(parts_ready, q * NSEG + s + 1)
                claim(b, q * STEPS + k)
                pe.matmul(scratch[:], pick[:, N + n:N + n + 1].to_broadcast([3 * BC, P]), parts[:, s % 2, :],
                          start=True, stop=True).then_inc(c_ready, 1)

            def sum_states(b, q, k):
                s, n = divmod(k, N)
                if n == 0:
                    wait(pe, gated, q * NSEG + s)
                    pe.wait_ge(du_ready, q * NSEG + s + 1)
                    for i in range(CB):
                        for h in range(NH):
                            pe.matmul(y_acc[:, i, h * P:(h + 1) * P], du[:, h, i * P:(i + 1) * P], ident[:],
                                      start=(i % 2 == 0 and h == 0), stop=False, is_transpose=True,
                                      skip_group_check=True)
                pe.wait_ge(ch_ready, q * STEPS + k + 1)
                for i in range(CB):
                    for h in range(NH):
                        mm = pe.matmul(y_acc[:, i, h * P:(h + 1) * P], state[:, k % 4, h, i * P:(i + 1) * P],
                                       ident[:], start=False, stop=(n == N - 1), is_transpose=True,
                                       skip_group_check=True)
                mm.then_inc(summed, 1)

            def scratch_tile(b, q, name, s, i):
                d, c = divmod(s, NC)
                if name == "xnT":
                    if i == 0:
                        pe.wait_ge(xn_ready, q + 1)
                    claim(b)
                    d, g = divmod(i, NC)
                    for j in range(CB):
                        r = g * CB + j
                        mm = pe.transpose(scratch[:, j * P:(j + 1) * P], xn[:, (BLK - 1 - r) if d else r, :],
                                          (flip if d else ident)[:])
                elif name == "u":
                    claim(b)
                    mm = pe.matmul(scratch[:], in_w[:, d, i * P:(i + 1) * P], xnT[:, d, c * CH:(c + 1) * CH],
                                   start=True, stop=True)
                elif name == "z":
                    claim(b)
                    for j in range(2):
                        t0 = c * CH + (2 * i + j) * P
                        mm = pe.matmul(scratch[:, j * DI:(j + 1) * DI], xnT[:, d, t0:t0 + P],
                                       in_w[:, d, DI:2 * DI], start=True, stop=True)
                elif name == "xdbl":
                    pe.wait_ge(uc_ready, q * NSEG + s + 1)
                    claim(b)
                    for h in range(NH):
                        mm = pe.matmul(scratch[0:XR, :], xproj[:, d, h, :], uc[:, h, :], start=(h == 0),
                                       stop=(h == NH - 1))
                elif name == "dt":
                    if i == 0:
                        pe.wait_ge(hi_ready, q * NSEG + s + 1)
                    claim(b)
                    mm = pe.matmul(scratch[:], dt_w[3 * BC:XR, d, i * P:(i + 1) * P], dt_low[3 * BC:XR, :],
                                   start=True, stop=True)
                elif name == "turn":
                    if i == 0:
                        pe.wait_ge(gated, q * NSEG + s + 1)
                    claim(b)
                    for j in range(CB):
                        at = CB - 1 - j if d else j
                        mm = pe.transpose(scratch[:, at * P:(at + 1) * P],
                                          gate[:, s % 2, j, i * P:(i + 1) * P], (flip if d else ident)[:])
                elif name == "out":
                    claim(b)
                    for j in range(CB):
                        for h in range(NH):
                            mm = pe.matmul(scratch[:, j * D:(j + 1) * D], y_turn[:, h, j * P:(j + 1) * P],
                                           out_w[:, d, h, :], start=(h == 0), stop=(h == NH - 1))
                elif name == "x1T":
                    if i == 0:
                        pe.wait_ge(x1_ready, q + 1)
                    claim(b)
                    for j in range(CB):
                        mm = pe.transpose(scratch[:, j * P:(j + 1) * P], x1[:, i * CB + j, :], ident[:])
                elif name == "logits":
                    claim(b)
                    for j in range(BLK):
                        mm = pe.matmul(scratch[:, j * E:(j + 1) * E], x1T[:, j * P:(j + 1) * P], wg[:],
                                       start=True, stop=True)
                elif name == "combT":
                    if i == 0:
                        pe.wait_ge(comb_ready, q + 1)
                    claim(b)
                    for j in range(CB):
                        mm = pe.matmul(scratch[0:E, j * P:(j + 1) * P], comb[:, i * CB + j, :], ident[:],
                                       start=True, stop=True)
                elif name == "b2":
                    claim(b)
                    for j in range(CB):
                        r = i * CB + j
                        mm = pe.matmul(scratch[:, j * D:(j + 1) * D], combT[:, r * P:(r + 1) * P], b2[:],
                                       start=True, stop=True)
                mm.then_inc(scratch_ready, 1)

            def ffn_tile(q, kind, sub):
                at = FFN_AT[(kind, sub)]
                if at >= FFN_BANKS:
                    old = FFN[at - FFN_BANKS]
                    pe.wait_ge(g_ready if old[0] == "g" else hg_ready, q * SUBS + old[1] + 1)
                u, j = divmod(sub, HB)
                c, e = divmod(u, E)
                pe.matmul(ffn_in[:, at % FFN_BANKS, :], (w1 if kind == "g" else w0)[:, e, j * P:(j + 1) * P],
                          x1T[:, c * CH:(c + 1) * CH], start=True, stop=True).then_inc(tile_ready, 1)

            def down(q, sub):
                u, j = divmod(sub, HB)
                pe.wait_ge(hg_ready, q * SUBS + sub + 1)
                if j == 0 and u:
                    wait(pe, unit_added, q * UNITS + u)
                for i in range(CB):
                    mm = pe.matmul(ffn_out[:, i, :], hg[:, sub % HG_SLOTS, i * P:(i + 1) * P], w2[:, u % E, j, :],
                                   start=(j == 0 and i == 0), stop=(j == HB - 1), skip_group_check=True)
                mm.then_inc(hg_used, 1)

            def iteration(b):
                claimed.clear()
                if not isinstance(b, int):
                    pe.wait_ge(ffn_loaded, 16 * len(ffn_loads))
                for name, off, *arg in events_of(b):
                    if name == "c_row":
                        c_row(b, b + off, *arg)
                    elif name == "b_row":
                        b_row(b + off, *arg)
                    elif name == "sum":
                        sum_states(b, b + off, *arg)
                    elif name in SCRATCH_TILES:
                        scratch_tile(b, b + off, name, *arg)
                    elif name == "gates":
                        for j in range(HB):
                            ffn_tile(b + off, "g", arg[0] * HB + j)
                    elif name == "hidden":
                        ffn_tile(b + off, "h", *arg)
                    elif name == "down":
                        down(b + off, *arg)

            pe.wait_ge(mamba_loaded, 16 * len(mamba_loads))
            iterations(pe, iteration)

        @block.scalar
        def _(act):
            def exp_ln_tables():
                act.preload_act_table_set(EXP_LN_TABLES)

            def copy_c(q, k):
                wait(act, ch_ready, q * STEPS + k - 3)
                act.wait_ge(c_ready, q * STEPS + k + 1)
                act.activation(c_rep[:, k % 4, :], scratch[:], ACT.Copy).then_inc(c_copied, 1)

            def decays(q, k):
                s, n = divmod(k, N)
                if n == 0:
                    act.wait_ge(dt_ready, q * NSEG + s + 1)
                wait(act, scan_ready, q * STEPS + k - 3)
                for h in range(NH):
                    e = act.activation(decay[:, k % 4, h, :], dt[:, s % 2, h, :], ACT.Exp,
                                       scale=a_neg[:, s // NC, h, n:n + 1])
                e.then_inc(decay_ready, 1)

            def root(b, event):
                nth = before(b, lambda i: len(norms_of(i))) + norms_of(b).index(event)
                act.wait_ge(var_ready, nth + 1)
                act.activation(rstd[:], var[:], ACT.Ln).then_inc(log_ready, 1)
                act.wait_ge(log_ready, nth + 1)
                act.activation(rstd[:], rstd[:], ACT.Exp, scale=-0.5).then_inc(root_ready, 1)

            def gates(q, u):
                if u >= 2:
                    wait(act, hg_ready, q * SUBS + (u - 1) * HB)
                for j in range(HB):
                    at = FFN_AT[("g", u * HB + j)]
                    act.wait_ge(tile_ready, q * 2 * SUBS + at + 1)
                    act.activation(g_act[:, u % 2, j, :], ffn_in[:, at % FFN_BANKS, :], ACT.Silu,
                                   bias=b1[:, u % E, j:j + 1]).then_inc(g_ready, 1)
                if FFN_FROM + 3 * u not in Z_SLOTS:
                    exp_ln_tables()

            def scratch_tile(b, q, event):
                name, off, s, i = event
                d, c = divmod(s, NC)
                if name != "b2":
                    tile_wait(act, b, event)
                if name == "xnT":
                    act.activation(xnT[:, i // NC, (i % NC) * CH:(i % NC + 1) * CH], scratch[:], ACT.Identity,
                                   bias=beta[:], scale=gamma[:]).then_inc(scratch_free, 1)
                elif name == "u":
                    wait(act, conv_ready, q * NSEG + s)
                    t0 = TAPS - 1 + c * CH
                    act.activation(u_pad[:, i, t0:t0 + CH], scratch[:], ACT.Copy).then_inc(scratch_free, 1)
                elif name == "z":
                    act.activation(gate[:, s % 2, 2 * i:2 * i + 2, :],
                                   scratch[:].rearrange("p (i e) -> p i e", i=2), ACT.Silu).then_inc(scratch_free, 1)
                    if i == 1:
                        act.wait_ge(conv_ready, q * NSEG + s + 1)
                        act.activation(uc[:], uc[:], ACT.Silu).then_inc(uc_ready, 1)
                        exp_ln_tables()
                elif name == "xdbl":
                    wait(act, summed_rows, q * NSEG + s - 1)
                    act.activation(rest[0:XR, :], scratch[0:XR, :], ACT.Copy).then_inc(scratch_free, 1)
                    left_wait(act, b, event)
                    act.activation(parts[:, s % 2, :], rest[0:3 * BC, :], ACT.Copy).then_inc(hi_ready, 1)
                elif name == "dt":
                    wait(act, drive_ready, q * STEPS + N * (s - 1))
                    act.activation(dtu[:, s % 2, i, :], scratch[:], ACT.Identity, bias=dt_b[:, d, i:i + 1])
                    act.activation(dt[:, s % 2, i, :], scratch[:], ACT.Abs,
                                   bias=dt_b[:, d, i:i + 1]).then_inc(scratch_free, 1)
                    if i == NH - 1:
                        left_wait(act, b, event)
                        act.activation(dt[:, s % 2], dt[:, s % 2], ACT.Exp, scale=-1.0).then_inc(exp_ready, 1)
                        act.wait_ge(exp_ready, q * NSEG + s + 1)
                        act.activation(dt[:, s % 2], dt[:, s % 2], ACT.Ln, bias=1.0).then_inc(soft_ready, 1)
                elif name == "turn":
                    act.activation(y_turn[:, i, :], scratch[:], ACT.Copy).then_inc(scratch_free, 1)
                elif name == "out":
                    act.activation(rest[:], scratch[:], ACT.Copy).then_inc(scratch_free, 1)
                elif name == "x1T":
                    act.activation(x1T[:, i * CH:(i + 1) * CH], scratch[:], ACT.Copy).then_inc(scratch_free, 1)
                elif name == "logits":
                    act.activation(logits[:], scratch[:, 0:BLK * E].rearrange("p (i e) -> p i e", i=BLK),
                                   ACT.Copy).then_inc(scratch_free, 1)
                elif name == "combT":
                    if not isinstance(b, int) or b < B:
                        wait(act, dtu_ready, b * NSEG + 2)
                    act.activation(combT[:, i * CH:(i + 1) * CH], scratch[0:E, :], ACT.Copy).then_inc(scratch_free, 1)

            def iteration(b):
                if not isinstance(b, int):
                    act.wait_ge(ffn_loaded, 16 * len(ffn_loads))
                for event in events_of(b):
                    name, off, *arg = event
                    if name == "c_row":
                        copy_c(b + off, *arg)
                    elif name == "decay":
                        decays(b + off, *arg)
                    elif name == "spread":
                        root(b, event)
                    elif name == "mid":
                        s = arg[0]
                        act.wait_ge(rest_ready, (b + off) * NSEG + s + 1)
                        act.activation(parts[BC:2 * BC, s % 2, :], rest[BC:2 * BC, :], ACT.Copy)
                        act.activation(mid[2 * BC:, :], rest[2 * BC:3 * BC, :], ACT.Copy).then_inc(mid_ready, 1)
                    elif name == "comb":
                        act.wait_ge(gap_ready, b + off + 1)
                        act.activation(ratio[:], gap[:], ACT.Exp).then_inc(ratio_ready, 1)
                    elif name == "gates":
                        gates(b + off, *arg)
                    elif name in SCRATCH_TILES:
                        scratch_tile(b, b + off, event)

            act.wait_ge(mamba_loaded, 16 * len(mamba_loads))
            exp_ln_tables()
            act.activation(a_exp[:], a_log[:], ACT.Exp).then_inc(a_ready, 1)
            act.wait_ge(a_ready, 1)
            act.activation(a_neg[:], a_exp[:], ACT.Copy, scale=-1.0).then_inc(a_ready, 1)
            act.wait_ge(a_ready, 2)
            iterations(act, iteration)

        @block.gpsimd
        def _(pool):
            pool.memset(one[:], 1.0).then_inc(one_ready, 1)
            pool.wait_ge(one_ready, 1)
            with pool.Fori(0, B) as b:
                for k in range(STEPS):
                    s, n = divmod(k, N)
                    pool.wait_ge(scan_ready, b * STEPS + k + 1)
                    pool.wait_ge(c_copied, b * STEPS + k + 1)
                    if s % NC < NC - 1:
                        pool.tensor_tensor(last[:, n, :], state[:, k % 4, :, CH - 1], one[:],
                                           ALU.mult).then_inc(last_ready, 1)
                        pool.wait_ge(last_ready, last_count(b, k))
                    pool.tensor_tensor(state[:, k % 4], state[:, k % 4],
                                       c_rep[:, k % 4:k % 4 + 1, :].to_broadcast([P, NH, CH]),
                                       ALU.mult).then_inc(ch_ready, 1)

        @block.vector
        def _(dve):
            linked = [0]

            def links(b):
                return sum(LINKS.get(e[0], 0) for e in events_of(b))

            def link(b, ins):
                linked[0] += 1
                ins.then_inc(chain, 1)
                dve.wait_ge(chain, before(b, links) + linked[0])

            def spread_over(v):
                return v[:].rearrange("p (i o) -> p i o", o=1).to_broadcast([P, BLK, E])

            def stats_of(b, q, which):
                if which == 0:
                    dve.wait_ge(x_loaded, 16 * (q + 1))
                elif which == 1:
                    dve.wait_ge(summed_rows, (q + 1) * NSEG)
                else:
                    dve.wait_ge(unit_added, (q + 1) * UNITS)
                for i in range(BLK):
                    ins = dve.bn_stats(stats[:, i, :], (xn, res, x1)[which][:, i, :])
                ins.then_inc(stats_ready, 1)

            def spread(b, event):
                nth = before(b, lambda i: len(norms_of(i))) + norms_of(b).index(event)
                dve.wait_ge(stats_ready, nth + 1)
                dve.tensor_tensor(mean[:], stats[:, :, 1], stats[:, :, 4], ALU.add)
                dve.tensor_tensor(apart[:], stats[:, :, 1], stats[:, :, 4], ALU.subtract)
                link(b, dve.tensor_tensor(var[:], stats[:, :, 2], stats[:, :, 5], ALU.add))
                dve.tensor_scalar(mean[:], mean[:], 0.5, None, ALU.mult)
                dve.tensor_scalar(var[:], var[:], 1.0 / D, EPS, ALU.mult, ALU.add)
                link(b, dve.scalar_tensor_tensor(apart[:], apart[:], 0.25, apart[:], ALU.mult, ALU.mult))
                dve.tensor_tensor(var[:], var[:], apart[:], ALU.add).then_inc(var_ready, 1)

            def normal(b, q, which, nth):
                dve.wait_ge(root_ready, nth + 1)
                link(b, dve.tensor_tensor(newton[:], var[:], rstd[:], ALU.mult))
                link(b, dve.tensor_tensor(newton[:], newton[:], rstd[:], ALU.mult))
                link(b, dve.tensor_scalar(newton[:], newton[:], -0.5, 1.5, ALU.mult, ALU.add))
                link(b, dve.tensor_tensor(rstd[:], rstd[:], newton[:], ALU.mult))
                src, dst, done = ((xn, xn, xn_ready), (res, x1, x1_ready), (x1, x1, rows_ready))[which]
                if which == 1:
                    dve.wait_ge(stored, 16 * (q + 1))
                for i in range(BLK):
                    ins = dve.tensor_scalar(dst[:, i, :], src[:, i, :], mean[:, i:i + 1], rstd[:, i:i + 1],
                                            ALU.subtract, ALU.mult)
                ins.then_inc(done, 1)

            def drive_step(q, k):
                s, n = divmod(k, N)
                if n == 0:
                    dve.wait_ge(dtu_ready, q * NSEG + s + 1)
                dve.wait_ge(b_ready, q * STEPS + k + 1)
                wait(dve, scan_ready, q * STEPS + k - 1)
                dve.tensor_tensor(drive[:, k % 2], dtu[:, s % 2],
                                  b_rep[:].rearrange("p (o t) -> p o t", o=1).to_broadcast([P, NH, CH]),
                                  ALU.mult).then_inc(drive_ready, 1)

            def scan_step(q, k):
                s, n = divmod(k, N)
                dve.wait_ge(drive_ready, q * STEPS + k + 1)
                dve.wait_ge(decay_ready, q * STEPS + k + 1)
                wait(dve, summed, q * STEPS + k - 3)
                if s % NC:
                    dve.wait_ge(last_ready, last_count(q, k - N))
                for h in range(NH):
                    ins = dve.tensor_tensor_scan(state[:, k % 4, h, :], decay[:, k % 4, h, :], drive[:, k % 2, h, :],
                                                 last[:, n, h:h + 1] if s % NC else 0.0, ALU.mult, ALU.add)
                ins.then_inc(scan_ready, 1)

            def convolve(b, q, s):
                d, c = divmod(s, NC)
                left_wait(dve, b, ("u", 1 if s == 0 else 0, s, 1))
                for t in reversed(range(TAPS)):
                    for h in range(NH):
                        taps = u_pad[:, h, c * CH + t:c * CH + t + CH]
                        w = conv_w[:, d, h, t:t + 1]
                        if t == TAPS - 1:
                            ins = dve.tensor_scalar(uc[:, h, :], taps, w, conv_b[:, d, h:h + 1], ALU.mult, ALU.add)
                        else:
                            ins = dve.scalar_tensor_tensor(uc[:, h, :], taps, w, uc[:, h, :], ALU.mult, ALU.add)
                    if t:
                        link(b, ins)
                ins.then_inc(conv_ready, 1)

            def times_u(q, s):
                dve.wait_ge(soft_ready, q * NSEG + s + 1)
                dve.scalar_tensor_tensor(dt[:, s % 2], dtu[:, s % 2], 0.0, dt[:, s % 2], ALU.max,
                                         ALU.add).then_inc(dt_ready, 1)
                dve.wait_ge(uc_ready, q * NSEG + s + 1)
                wait(dve, summed, q * STEPS + N * (s - 1) + 1)
                for h in range(NH):
                    ins = dve.tensor_scalar(du[:, h, :], uc[:, h, :], d_skip[:, s // NC, h:h + 1], None, ALU.mult)
                ins.then_inc(du_ready, 1)
                dve.wait_ge(dt_ready, q * NSEG + s + 1)
                dve.tensor_tensor(dtu[:, s % 2], dt[:, s % 2], uc[:], ALU.mult).then_inc(dtu_ready, 1)

            def hidden(q, sub):
                u, j = divmod(sub, HB)
                at = FFN_AT[("h", sub)]
                dve.wait_ge(tile_ready, q * 2 * SUBS + at + 1)
                dve.wait_ge(g_ready, q * SUBS + sub + 1)
                if sub >= HG_SLOTS:
                    wait(dve, hg_used, q * SUBS + sub + 1 - HG_SLOTS)
                dve.scalar_tensor_tensor(hg[:, sub % HG_SLOTS, :], ffn_in[:, at % FFN_BANKS, :], b0[:, u % E, j:j + 1],
                                         g_act[:, u % 2, j, :], ALU.add, ALU.mult).then_inc(hg_ready, 1)

            def add_unit(b, q, u):
                c, e = divmod(u, E)
                dve.wait_ge(hg_used, q * SUBS + HB * (u + 1))
                if u:
                    wait(dve, unit_added, q * UNITS + u)
                else:
                    left_wait(dve, b, ("b2", -1, 0, 1))
                for i in range(CB):
                    r = c * CB + i
                    ins = dve.scalar_tensor_tensor(x1[:, r, :], ffn_out[:, i, :], comb[:, r, e:e + 1], x1[:, r, :],
                                                   ALU.mult, ALU.add)
                ins.then_inc(unit_added, 1)

            def first_best(b, of, best, mask):
                link(b, dve.tensor_reduce(best[:], of[:], AX_X, ALU.max))
                link(b, dve.tensor_tensor(mask[:], of[:], spread_over(best), ALU.is_equal))
                link(b, dve.tensor_tensor(mask[:], mask[:], prio[:].rearrange("p (o e) -> p o e", o=1)
                                          .to_broadcast([P, BLK, E]), ALU.mult))
                link(b, dve.tensor_reduce(vmax[:], mask[:], AX_X, ALU.max))
                link(b, dve.tensor_tensor(mask[:], mask[:], spread_over(vmax), ALU.is_equal))

            def best_two(b):
                left_wait(dve, b, ("logits", -1, 0, 0))
                link(b, dve.tensor_tensor(logits[:], logits[:], bg[:].rearrange("p (o e) -> p o e", o=1)
                                          .to_broadcast([P, BLK, E]), ALU.add))
                first_best(b, logits, m1, first)
                link(b, dve.scalar_tensor_tensor(work[:], first[:], NEG, logits[:], ALU.mult, ALU.add))
                first_best(b, work, m2, second)
                dve.tensor_tensor(gap[:], m2[:], m1[:], ALU.subtract).then_inc(gap_ready, 1)

            def shares(b, q):
                dve.wait_ge(ratio_ready, q + 1)
                link(b, dve.tensor_scalar(wsum[:], ratio[:], 1.0, None, ALU.add))
                link(b, dve.reciprocal(weight1[:], wsum[:]))
                link(b, dve.tensor_tensor(weight2[:], weight1[:], ratio[:], ALU.mult))
                link(b, dve.tensor_tensor(first[:], first[:], spread_over(weight1), ALU.mult))
                link(b, dve.tensor_tensor(second[:], second[:], spread_over(weight2), ALU.mult))
                dve.tensor_tensor(comb[:], first[:], second[:], ALU.add).then_inc(comb_ready, 1)

            def scratch_rows(i):
                return scratch[:].rearrange("p (i e) -> p i e", i=i)

            def iteration(b):
                linked[0] = 0
                if not isinstance(b, int):
                    dve.wait_ge(ffn_loaded, 16 * len(ffn_loads))
                for event in events_of(b):
                    name, off, *arg = event
                    q = b + off
                    if name == "drive":
                        drive_step(q, *arg)
                    elif name == "scan":
                        scan_step(q, *arg)
                    elif name == "stats":
                        stats_of(b, q, arg[1])
                    elif name == "spread":
                        spread(b, event)
                    elif name == "normal":
                        nth = before(b, lambda i: len(norms_of(i))) + norms_of(b).index(("spread", off, *arg))
                        normal(b, q, arg[1], nth)
                    elif name == "conv":
                        convolve(b, q, arg[0])
                    elif name == "rest":
                        s = arg[0]
                        dve.wait_ge(hi_ready, q * NSEG + s + 1)
                        dve.tensor_tensor(rest[0:3 * BC, :], rest[0:3 * BC, :], parts[:, s % 2, :],
                                          ALU.subtract).then_inc(rest_ready, 1)
                    elif name == "low":
                        s = arg[0]
                        dve.wait_ge(mid_ready, q * NSEG + s + 1)
                        dve.tensor_tensor(parts[2 * BC:, s % 2, :], rest[2 * BC:3 * BC, :], mid[2 * BC:, :],
                                          ALU.subtract).then_inc(parts_ready, 1)
                    elif name == "dtu":
                        times_u(q, arg[0])
                    elif name == "gate":
                        s = arg[0]
                        dve.wait_ge(summed, q * STEPS + N * (s + 1))
                        for g in range(2):
                            ins = dve.tensor_tensor(gate[:, s % 2, 2 * g:2 * g + 2, :], y_acc[:, 2 * g:2 * g + 2, :],
                                                    gate[:, s % 2, 2 * g:2 * g + 2, :], ALU.mult)
                        ins.then_inc(gated, 1)
                    elif name == "residual":
                        d, c = divmod(arg[0], NC)
                        at = CB * (NC - 1 - c if d else c)
                        dve.wait_ge(res_loaded, 16 * (q + 1))
                        if d:
                            wait(dve, summed_rows, q * NSEG + arg[0])
                        left_wait(dve, b, ("out", off, *arg))
                        dve.scalar_tensor_tensor(res[:, at:at + CB, :], res[:, at:at + CB, :], 1.0 if d else 2.0,
                                                 rest[:].rearrange("p (i e) -> p i e", i=CB), ALU.mult,
                                                 ALU.add).then_inc(summed_rows, 1)
                    elif name == "best":
                        best_two(b)
                    elif name == "comb":
                        shares(b, q)
                    elif name == "b2":
                        tile_wait(dve, b, event)
                        rows = x1[:, arg[1] * CB:(arg[1] + 1) * CB, :]
                        dve.tensor_tensor(rows, scratch_rows(CB), rows, ALU.add).then_inc(scratch_free, 1)
                    elif name == "product":
                        hidden(q, *arg)
                    elif name == "add":
                        add_unit(b, q, *arg)
                assert not isinstance(b, int) or linked[0] == links(b), (linked, links(b))

            dve.memset(u_pad[:, :, 0:TAPS - 1], 0.0).then_inc(pad_ready, 1)
            dve.wait_ge(pad_ready, 1)
            dve.wait_ge(mamba_loaded, 16 * len(mamba_loads))
            iterations(dve, iteration)


def kernel(**inputs):
    import numpy as _np
    import concourse.bacc as _bacc
    from concourse import mybir as _mybir
    from concourse.bass_utils import run_bass_kernel_spmd as _run

    def flat(v):
        return _np.ascontiguousarray(v)

    laid = {"x": flat(inputs["L0_attn_x"]), "gamma": flat(inputs["L0_attn_gamma"]), "beta": flat(inputs["L0_attn_beta"])}
    for d in ("f_", "b_"):
        pre = "L0_attn_" + d
        for name in ("in_w", "xproj_w", "dt_w", "out_w"):
            laid[d + name] = flat(_np.asarray(inputs[pre + name]).T)
        laid[d + "conv_w"] = flat(_np.asarray(inputs[pre + "conv_w"])[:, 0, :])
        laid[d + "A_log"] = flat(inputs[pre + "A_log"])
        for name in ("conv_b", "dt_b", "D"):
            laid[d + name] = flat(_np.asarray(inputs[pre + name]).reshape(NH, P).T)
    for name in ("Wg", "bg", "W0", "W1", "W2", "b2"):
        laid[name] = flat(inputs["L0_ffn_" + name])
    for name in ("b0", "b1"):
        laid[name] = flat(_np.asarray(inputs["L0_ffn_" + name]).reshape(E, HB, P).transpose(2, 0, 1))
    laid["ident"] = _np.eye(P, dtype=_np.float32)
    laid["flip"] = flat(_np.eye(P, dtype=_np.float32)[::-1])
    rows = _np.arange(3 * BC)[:, None] % BC == _np.arange(BC)[None, :]
    import ml_dtypes as _ml
    laid["pick"] = flat(rows.astype(_ml.bfloat16))
    laid["prio"] = flat(_np.broadcast_to(_np.arange(E, 0, -1, dtype=_np.float32), (P, E)))

    nc = _bacc.Bacc("TRN2", target_bir_lowering=False, num_devices=1)
    arrays, args = {}, {}
    for name, v in laid.items():
        arrays[f"in_{name}"] = v
        args[name] = nc.dram_tensor(f"in_{name}", v.shape, _mybir.dt.from_np(v.dtype), kind="ExternalInput").ap()
    out = nc.dram_tensor("out_0", (B, L, D), F32, kind="ExternalOutput").ap()
    build(nc, args, out)
    r = _run(nc, [arrays], core_ids=[0])
    return r.results[0]["out_0"]
```
